# Optimizing a Trainium2 kernel written in Bass

```python
import numpy as np
import jax
import jax.numpy as jnp

def _softmax(x, axis=-1):
    return jax.nn.softmax(x, axis=axis)

def _gelu(x):
    return jax.nn.gelu(x, approximate=True)

def _silu(x):
    return jax.nn.silu(x)

def _sigmoid(x):
    return jax.nn.sigmoid(x)

def _layernorm(x, axis=-1, eps=1e-05):
    m = jnp.mean(x, axis=axis, keepdims=True)
    v = jnp.var(x, axis=axis, keepdims=True)
    return (x - m) / jnp.sqrt(v + eps)

def _scatter_add(tgt, idx, src, axis=0):
    return tgt.at[idx].add(src)

def _segment_sum(src, seg, n):
    return jax.ops.segment_sum(src, seg, n)
kernel_name = 'mk_adj_preln_d2_adj_r2_510ff8'

def setup_inputs(seed: int=0):
    np.random.seed(seed)
    _w = jnp.asarray

    def _rec_inputs():
        import jax
        import jax.numpy as jnp
        _gk = jax.random.key(seed)
        x = -0.000929 + 1 * jax.random.normal(jax.random.fold_in(_gk, 1), (4096, 128), jnp.float32)
        _a = jax.random.bernoulli(jax.random.fold_in(_gk, 2), 0.00390625, (4096, 4096))
        _a = jnp.logical_or(_a, jnp.eye(4096, dtype=bool))
        _af = _a.astype(jnp.float32)
        _af = _af * jax.random.uniform(jax.random.fold_in(_gk, 3), (4096, 4096), jnp.float32, 0.05, 1)
        adj = _af
        return (x, adj)
    x, adj = _rec_inputs()

    def _L0_gnn_setup():
        import jax, jax.numpy as jnp
        import numpy as np
        N = 4096
        H = 128
        key = jax.random.key(seed)
        k_x, k_A, k_W = jax.random.split(key, 3)
        x = jax.random.normal(k_x, (N, H), dtype=jnp.float32)
        A = jax.random.uniform(k_A, (N, N), dtype=jnp.float32)
        alpha = jnp.array([0.5], dtype=jnp.float32)
        bound = 1.0 / np.sqrt(H)
        W = jax.random.uniform(k_W, (H, H), dtype=jnp.float32, minval=-bound, maxval=bound)
        b = jnp.zeros((H,), dtype=jnp.float32)
        t = jnp.zeros((1,), dtype=jnp.float32)
        return {'t': t, 'x': x, 'A': A, 'alpha': alpha, 'W': W, 'b': b}
    _L0_gnn_all = _L0_gnn_setup()
    _L0_gnn_in = {k: v for k, v in _L0_gnn_all.items() if k in ('t', 'alpha', 'W', 'b')}
    del _L0_gnn_all

    def _L1_gnn_setup():
        import jax, jax.numpy as jnp
        import numpy as np

        def _lap_mul(A, x):
            d = 1.0 / jnp.sqrt(jnp.sum(A, axis=-1))
            return d[:, None] * (A @ (d[:, None] * x))
        key = jax.random.key(seed)
        k1, k2, k3, k4, k5, k6 = jax.random.split(key, 6)
        N, D_IN, D_OUT = (2048, 128, 128)
        x = jax.random.normal(k1, (N, D_IN), dtype=jnp.float32)
        A = jax.random.uniform(k2, (N, N), dtype=jnp.float32)
        s1 = 1.0 / np.sqrt(D_IN)
        W1 = jax.random.uniform(k3, (D_IN, D_OUT), minval=-s1, maxval=s1, dtype=jnp.float32)
        b1 = jax.random.uniform(k4, (D_OUT,), minval=-s1, maxval=s1, dtype=jnp.float32)
        W2 = jax.random.uniform(k5, (D_IN, D_OUT), minval=-s1, maxval=s1, dtype=jnp.float32)
        b2 = jax.random.uniform(k6, (D_OUT,), minval=-s1, maxval=s1, dtype=jnp.float32)
        return {'x': x, 'A': A, 'W1': W1, 'b1': b1, 'W2': W2, 'b2': b2, 'sigma': 1, 'k': 4}
    _L1_gnn_all = _L1_gnn_setup()
    _L1_gnn_in = {k: v for k, v in _L1_gnn_all.items() if k in ('W1', 'b1', 'W2', 'b2')}
    del _L1_gnn_all
    return {'x': x, 'adj': adj, 'L0_gnn_t': _L0_gnn_in['t'], 'L0_gnn_alpha': _L0_gnn_in['alpha'], 'L0_gnn_W': _L0_gnn_in['W'], 'L0_gnn_b': _L0_gnn_in['b'], 'L1_gnn_W1': _L1_gnn_in['W1'], 'L1_gnn_b1': _L1_gnn_in['b1'], 'L1_gnn_W2': _L1_gnn_in['W2'], 'L1_gnn_b2': _L1_gnn_in['b2']}

def reference(x, adj, L0_gnn_t, L0_gnn_alpha, L0_gnn_W, L0_gnn_b, L1_gnn_W1, L1_gnn_b1, L1_gnn_W2, L1_gnn_b2):
    import jax
    import jax.numpy as jnp

    def _L0_gnn_ref(t, x, A, alpha, W, b):
        import jax, jax.numpy as jnp
        import numpy as np
        N = 4096
        H = 128
        a = alpha[0]
        A_prime = a * A
        diag = jnp.diagonal(A_prime) + (1.0 - a)
        A_prime = A_prime.at[jnp.arange(N), jnp.arange(N)].set(diag)
        out_degree = A_prime.sum(axis=1)
        inv_deg = jnp.where(out_degree == 0.0, 0.0, 1.0 / out_degree)
        x = inv_deg[:, None] * A_prime @ x
        x = x @ W.T + b
        return jax.nn.relu(x)

    def _L1_gnn_ref(x, A, W1, b1, W2, b2, sigma, k):
        import jax, jax.numpy as jnp
        import numpy as np

        def _lap_mul(A, x):
            d = 1.0 / jnp.sqrt(jnp.sum(A, axis=-1))
            return d[:, None] * (A @ (d[:, None] * x))
        z = _lap_mul(A, x) @ W1 + b1
        z = jax.nn.leaky_relu(z, negative_slope=0.1)
        sq = jnp.sum(z * z, axis=-1)
        d2 = sq[:, None] + sq[None, :] - 2.0 * (z @ z.T)
        d2 = jnp.maximum(d2, 0.0)
        S = jnp.sqrt(d2 + 1e-10)
        S = jnp.exp(-S / (2.0 * sigma))
        order = jnp.argsort(-S, axis=-1)
        ranks = jnp.argsort(order, axis=-1)
        S = jnp.where(ranks < k, S, 0.0)
        A2 = S + A
        out = _lap_mul(A2, x) @ W2 + b2
        return out
    h = jnp.maximum(_layernorm(x, axis=-1), 0.0)
    x = x + _L0_gnn_ref(L0_gnn_t, h, adj, L0_gnn_alpha, L0_gnn_W, L0_gnn_b)
    h = jnp.maximum(_layernorm(x, axis=-1), 0.0)
    x = x + _L1_gnn_ref(h, adj, L1_gnn_W1, L1_gnn_b1, L1_gnn_W2, L1_gnn_b2, 1, 4)
    return x

_drawn_inputs = setup_inputs


def setup_inputs(seed=0):
    import zlib

    import numpy as np

    out = dict(_drawn_inputs(seed))
    spreads = {'L0_gnn_b': (0.0, 0.1)}
    factors = {'L1_gnn_b1': 2.767}
    for name, (base, spread) in spreads.items():
        noise = np.random.default_rng([zlib.crc32(name.encode()), seed]).standard_normal(out[name].shape)
        drawn = base * np.exp(spread * noise) if base else spread * noise
        out[name] = jnp.asarray(drawn.astype(out[name].dtype))
    for name, factor in factors.items():
        out[name] = (out[name] * factor).astype(out[name].dtype)
    return out
```

```python
from contextlib import ExitStack

import concourse.bass as bass
from concourse import mybir

F32 = mybir.dt.float32
F32R = mybir.dt.float32r
U32 = mybir.dt.uint32
ALU = mybir.AluOpType
ACT = mybir.ActivationFunctionType
AX = mybir.AxisListType

P = 128
CHUNK = 512
K = CHUNK // P
SLOTS = 4
NEAR = 4
TOP = 8
LN_EPS = 1e-5
SIM_EPS = 1e-10
LEAK = 0.1
DMA = 16


def graph_layers(nc, x_d, at_d, alpha_d, wt_d, b_d, w1_d, b1_d, w2_d, b2_d, ident_d, out_d, u_d):
    N, H = x_d.shape
    TILES = N // P
    CHUNKS = N // CHUNK
    GROUPS = TILES // K
    LAPS = GROUPS // SLOTS
    SWEEP = CHUNKS * GROUPS
    PAIRS = CHUNKS // 2
    assert H == P and CHUNKS % 2 == 0 and GROUPS == LAPS * SLOTS and PAIRS * 2 == 8

    x_tiles = x_d.rearrange("(t p) f -> p t f", p=P)
    out_tiles = out_d.rearrange("(t p) f -> p t f", p=P)
    u_tiles = u_d.rearrange("(t p) f -> p t f", p=P)

    with ExitStack() as ctx:
        def sb(name, shape, dt=F32):
            return ctx.enter_context(nc.sbuf_tensor(name, shape, dt))

        def sem(name):
            return ctx.enter_context(nc.semaphore(name))

        x_sb = sb("x_sb", [P, TILES, P])
        h1 = sb("h1", [P, TILES, P])
        feat_a = sb("feat_a", [P, TILES, P])
        ring = sb("ring", [P, SLOTS, K, CHUNK])
        ident = sb("ident", [P, P])
        ones = sb("ones", [P, P])
        wt = sb("wt", [P, P])
        w1 = sb("w1", [P, P])
        w2 = sb("w2", [P, P])
        b_row = sb("b_row", [P, P])
        b1_row = sb("b1_row", [P, P])
        b2_row = sb("b2_row", [P, P])
        alpha = sb("alpha", [P, 1])
        beta = sb("beta", [P, 1])
        neg_half = sb("neg_half", [P, TILES])
        half = sb("half", [P, K, NEAR])
        stats = sb("stats", [P, TILES, 6])
        mean_var = sb("mean_var", [P, TILES, 2])
        var_eps = sb("var_eps", [P, TILES])
        rstd0 = sb("rstd0", [P, TILES])
        deg = sb("deg", [P, TILES])
        d_col = sb("d_col", [P, TILES])
        d2_col = sb("d2_col", [P, TILES])
        sq_col = sb("sq_col", [P, TILES])
        sim = sb("sim", [P, TILES, NEAR])
        near = sb("near", [P, TILES, NEAR], U32)
        pow_in = sb("pow_in", [P, 2, K])
        pow_out = sb("pow_out", [P, 2, K])
        out_deg = sb("out_deg", [P, K])
        deg_zero = sb("deg_zero", [P, K])
        deg_safe = sb("deg_safe", [P, K])
        inv_deg = sb("inv_deg", [P, K])
        prod_t = sb("prod_t", [P, CHUNK])
        deg_part = sb("deg_part", [P, CHUNK])
        work = sb("work", [P, K, P])
        norm = sb("norm", [P, K, P])
        square = sb("square", [P, K, P])
        z_sq_t = sb("z_sq_t", [P, CHUNK])
        z_hi_now = sb("z_hi_now", [P, K, P], F32R)
        z_lo_now = sb("z_lo_now", [P, K, P], F32R)
        pick = sb("pick", [P, P], F32R)
        top8 = sb("top8", [P, K, TOP])
        idx8 = sb("idx8", [P, K, TOP], U32)
        dist_in = sb("dist_in", [P, K, NEAR])
        dist = sb("dist", [P, K, NEAR])
        sim_sum = sb("sim_sum", [P, K])
        sim_deg = sb("sim_deg", [P, K])
        idx_now = sb("idx_now", [P, 2, K * NEAR], U32)

        KB = 1024
        arena = sb("arena", [P, 80 * KB // 4])
        arena_at = nc.sbuf_base - 80 * KB

        def region(name, offset, shape, dt=F32):
            return nc.alloc_sbuf_tensor_at(name, shape, dt, offset=arena_at + offset)

        feat_b = region("feat_b", 0, [P, TILES, P])
        h_t = region("h_t", 16 * KB, [P, N])
        rows = region("rows", 0, [P, 2, N])
        z_hi = region("z_hi", 32 * KB, [P, N], F32R)
        z_lo = region("z_lo", 48 * KB, [P, N], F32R)
        acc = region("acc", 64 * KB, [P, K, CHUNK])
        z_norm = region("z_norm", 64 * KB, [P, N], F32R)
        gathered = region("gathered", 32 * KB, [P, 2, K * NEAR, P])
        near_sum = region("near_sum", 48 * KB, [P, K, P])
        x1_b2 = region("x1_b2", 50 * KB, [P, K, P])
        out_sb = region("out_sb", 52 * KB, [P, 2, K, P])

        psum = ctx.enter_context(nc.psum_tensor("psum", [P, 8, CHUNK], F32))
        BANK_W, BANK_DEG, BANK_T, BANK_Q = 2, 3, 4, 5
        ps_w = psum[:, BANK_W, :].rearrange("p (k f) -> p k f", k=K)
        ps_deg = psum[:, BANK_DEG, 0:K]
        ps_t = psum[:, BANK_T, :]
        ps_q = psum[:, BANK_Q, :]

        x_in = sem("x_in")
        small_in = [sem(f"small_in{i}") for i in range(8)]
        load_done = [sem(f"load_done{s}") for s in range(SLOTS)]
        pe_groups = sem("pe_groups")
        dve_groups = sem("dve_groups")
        unread = sem("unread")
        consts = sem("consts")
        var_ready = sem("var_ready")
        rstd_ready = sem("rstd_ready")
        h_norm = sem("h_norm")
        h_ready = sem("h_ready")
        ht_psum = sem("ht_psum")
        ht_ready = sem("ht_ready")
        prod_ready = sem("prod_ready")
        y1_ready = sem("y1_ready")
        y_ready = sem("y_ready")
        w_ready = sem("w_ready")
        w_used = sem("w_used")
        pow_wanted = sem("pow_wanted")
        pow_ready = sem("pow_ready")
        norm_ready = sem("norm_ready")
        h1_ready = sem("h1_ready")
        z_ready = sem("z_ready")
        sq_ready = sem("sq_ready")
        zt_psum = sem("zt_psum")
        zt_split = sem("zt_split")
        z_done = sem("z_done")
        q_psum = sem("q_psum")
        q_split = sem("q_split")
        q_done = sem("q_done")
        z_staged = sem("z_staged")
        pair_ready = sem("pair_ready")
        pair_free = sem("pair_free")
        row_ready = sem("row_ready")
        row_free = sem("row_free")
        dist_wanted = sem("dist_wanted")
        dist_ready = sem("dist_ready")
        sim_ready = sem("sim_ready")
        deg2_wanted = sem("deg2_wanted")
        feat_ready = sem("feat_ready")
        u_stored = sem("u_stored")
        idx_ready = sem("idx_ready")
        rows_in = [sem(f"rows_in{s}") for s in range(2)]
        near_ready = sem("near_ready")
        stored = [sem(f"stored{s}") for s in range(2)]

        def free_at_first(eng, *whats):
            for what in whats:
                eng.sem_inc(what, 1)

        def tiles(t, c):
            return t[:, bass.ds(c * K, K)] if not isinstance(c, int) else t[:, c * K:(c + 1) * K]

        def tile_at(t, i):
            return t[:, bass.ds(i, 1)] if not isinstance(i, int) else t[:, i:i + 1]

        def cols(t, c):
            return t[:, bass.ds(c * CHUNK, CHUNK)] if not isinstance(c, int) else t[:, c * CHUNK:(c + 1) * CHUNK]

        def over_features(v):
            return v.unsqueeze(2).to_broadcast([P, K, P])

        def over_tiles(v):
            return v.unsqueeze(1).to_broadcast([P, K, P])

        def wait_apart(eng, what, value):
            eng.wait_ge(what, value)
            eng.sem_inc(unread, 1)

        def tiles_of(d, c):
            return tiles(d, c)

        block = ctx.enter_context(nc.Block())

        @block.sync
        def _(sp):
            for g in range(GROUPS):
                sp.dma_start(x_sb[:, g * K:(g + 1) * K, :], x_tiles[:, g * K:(g + 1) * K, :]).then_inc(x_in, DMA)

            def load(sweep, c, g):
                n = c * GROUPS + g + sweep * SWEEP
                if sweep or not isinstance(c, int) or n >= SLOTS:
                    sp.wait_ge(pe_groups, n - SLOTS + 1)
                    if sweep == 0:
                        sp.wait_ge(dve_groups, n - SLOTS + 1)
                    elif sweep == 1 and isinstance(c, int):
                        sp.wait_ge(dve_groups, min(SWEEP, n - SLOTS + 1))
                sp.dma_start(ring[:, g % SLOTS].rearrange("p k n -> p (k n)"),
                             at_d[c, g]).then_inc(load_done[g % SLOTS], DMA)

            for sweep in range(3):
                for g in range(GROUPS):
                    load(sweep, 0, g)
                with sp.Fori(1, CHUNKS) as c:
                    for g in range(GROUPS):
                        load(sweep, c, g)

        def arrived(eng, sweep, c, g):
            eng.wait_ge(load_done[g % SLOTS], (c * LAPS + g // SLOTS + 1 + sweep * CHUNKS * LAPS) * DMA)

        @block.tensor
        def _(pe):
            def transposes(g):
                pe.wait_ge(h_ready, g + 1)
                if g >= 2:
                    pe.wait_ge(ht_ready, g - 1)
                for k in range(K):
                    last = nc.tensor.transpose(psum[:, BANK_T + g % 2, k * P:(k + 1) * P], feat_a[:, g * K + k, :], ident[:, :])
                last.then_inc(ht_psum, 1)

            def stream(sweep, c, par, feat, between):
                first = isinstance(c, int) and c == 0
                for g in range(GROUPS):
                    if sweep == 0 and first:
                        transposes(g)
                    if sweep == 1 and first:
                        pe.wait_ge(h1_ready, g + 2)
                    if sweep == 2 and first:
                        pe.wait_ge(feat_ready, g + 1)
                    arrived(pe, sweep, c, g)
                    for k in range(K):
                        t = g * K + k
                        last = nc.tensor.matmul(psum[:, par, :], feat[:, t, :], ring[:, g % SLOTS, k, :],
                                                start=(t == 0), stop=(t == TILES - 1 and sweep < 2),
                                                skip_group_check=(sweep == 2))
                    last.then_inc(pe_groups, 1)
                    if between is not None:
                        between(g)

            def weights(n, rhs):
                pe.wait_ge(w_used, n + 1)
                for k in range(K):
                    last = nc.tensor.matmul(ps_w[:, k, :], prod_t[:, k * P:(k + 1) * P], rhs[:, :], start=True, stop=True)
                return last

            def finish1(c, g):
                if g == 1:
                    pe.wait_ge(y1_ready, c + 1)
                    weights(c, wt)
                    for k in range(K):
                        last = nc.tensor.matmul(ps_deg[:, k:k + 1], deg_part[:, k * P:(k + 1) * P], ones[:, 0:1], start=True, stop=True)
                    last.then_inc(w_ready, 1)

            def finish2(c, g):
                if g == 1:
                    pe.wait_ge(y_ready, c + 1)
                    weights(c + CHUNKS, w1).then_inc(w_ready, 1)
                if g == 3:
                    pe.wait_ge(z_ready, c + 1)
                    pe.wait_ge(z_done, c + 1)
                    for k in range(K):
                        last = nc.tensor.transpose(ps_t[:, k * P:(k + 1) * P], norm[:, k, :], ident[:, :])
                    last.then_inc(zt_psum, 1)
                if g == 5:
                    pe.wait_ge(zt_split, c + 1)
                    pe.wait_ge(q_done, c + 1)
                    nc.tensor.matmul(ps_q, ones[:, :], z_sq_t[:, :], start=True, stop=True).then_inc(q_psum, 1)

            def finish3(c, par, g):
                if g == 4:
                    pe.wait_ge(near_ready, c + 1)
                    for k in range(K):
                        last = nc.tensor.matmul(psum[:, par, k * P:(k + 1) * P], near_sum[:, k, :], ident[:, :],
                                                start=False, stop=(k == K - 1), skip_group_check=True)
                    last.then_inc(prod_ready, 1)
                if g == 6:
                    pe.wait_ge(y_ready, c + CHUNKS + 1)
                    weights(c + 2 * CHUNKS, w2).then_inc(w_ready, 1)

            def run_sweep(sweep, feat, before, finish):
                stream(sweep, 0, 0, feat, before)
                with pe.Fori(0, CHUNKS // 2 - 1) as i:
                    stream(sweep, i * 2 + 1, 1, feat, lambda g: finish(i * 2, 0, g))
                    stream(sweep, i * 2 + 2, 0, feat, lambda g: finish(i * 2 + 1, 1, g))
                stream(sweep, CHUNKS - 1, 1, feat, lambda g: finish(CHUNKS - 2, 0, g))

            free_at_first(pe, zt_psum, q_psum, prod_ready)
            for i in range(1, 8):
                pe.wait_ge(small_in[i], DMA)
            pe.wait_ge(consts, 1)
            run_sweep(0, feat_a, None, lambda c, par, g: finish1(c, g))
            run_sweep(1, feat_b, lambda g: finish1(CHUNKS - 1, g), lambda c, par, g: finish2(c, g))
            for g in range(GROUPS):
                finish2(CHUNKS - 1, g)

            pe.wait_ge(z_done, CHUNKS + 1)
            pe.wait_ge(q_done, CHUNKS + 1)
            pe.wait_ge(w_used, 2 * CHUNKS + 1)
            with pe.Fori(0, GROUPS) as i:
                for k in range(K):
                    pe.wait_ge(z_staged, i * K + (k + 1))
                    for q in range(PAIRS):
                        pe.wait_ge(pair_free, (i * K + k) * PAIRS + (q + 1))
                        parts = ((pick[:, :], z_norm), (z_hi_now[:, k, :], z_hi), (z_hi_now[:, k, :], z_lo),
                                 (z_lo_now[:, k, :], z_hi))
                        for m, (lhs, rhs) in enumerate(parts):
                            for b in range(2):
                                last = nc.tensor.matmul(psum[:, 2 * q + b, :], lhs, cols(rhs, 2 * q + b),
                                                        start=(m == 0), stop=(m == len(parts) - 1))
                        last.then_inc(pair_ready, 1)
            pe.wait_ge(pair_free, (TILES + 1) * PAIRS)

            run_sweep(2, feat_a, None, finish3)
            for g in range(GROUPS):
                finish3(CHUNKS - 1, 1, g)

        @block.scalar
        def _(act):
            for i, (to, of) in enumerate(((alpha, alpha_d), (ident, ident_d), (wt, wt_d), (w1, w1_d), (w2, w2_d),
                                          (b_row, b_d), (b1_row, b1_d), (b2_row, b2_d))):
                act.dma_start(to[:, :], of).then_inc(small_in[i], DMA)

            free_at_first(act, h1_ready, sq_ready)
            for par in range(2):
                act.sem_inc(stored[par], DMA)

            def h_of(g):
                act.wait_ge(h_norm, g + 1)
                nc.scalar.activation(feat_a[:, g * K:(g + 1) * K, :], h1[:, g * K:(g + 1) * K, :], ACT.Relu).then_inc(h_ready, 1)

            def ht_of(g):
                act.wait_ge(ht_psum, g + 1)
                nc.scalar.activation(cols(h_t, g), psum[:, BANK_T + g % 2, :], ACT.Copy, scale=beta[:, 0:1]).then_inc(ht_ready, 1)

            for g in range(GROUPS):
                h_of(g)
                if g >= 1:
                    ht_of(g - 1)
            ht_of(GROUPS - 1)

            with act.Fori(0, CHUNKS) as c:
                act.wait_ge(norm_ready, c + 1)
                nc.scalar.activation(tiles(h1, c), norm[:, :, :], ACT.Relu)
                nc.scalar.activation(tiles(d_col, c), pow_out[:, 1, :], ACT.Copy)
                for k in range(K):
                    last = nc.scalar.activation(tile_at(feat_b, c * K + k)[:, 0], norm[:, k, :], ACT.Relu, scale=pow_out[:, 1, k:k + 1])
                last.then_inc(h1_ready, 1)

            def product(sweep, c, par, done, value):
                act.wait_ge(done, value)
                act.wait_ge(w_ready, c + sweep * CHUNKS)
                nc.scalar.activation(prod_t[:, :], psum[:, par, :], ACT.Copy).then_inc(y_ready, 1)

            with act.Fori(0, CHUNKS // 2) as i:
                for par in range(2):
                    c = i * 2 + par
                    product(1, c, par, pe_groups, c * GROUPS + SWEEP + GROUPS)
                    act.drain()
                    wait_apart(act, z_ready, c + 1)
                    for k in range(K):
                        last = nc.scalar.activation(square[:, k, :], norm[:, k, :], ACT.Square,
                                                    accum_out=tile_at(sq_col, c * K + k))
                    last.then_inc(sq_ready, 1)
                    act.wait_ge(zt_psum, c + 2)
                    act.wait_ge(q_psum, c + 1)
                    nc.scalar.activation(cols(z_hi, c), ps_t, ACT.Copy)
                    nc.scalar.activation(z_sq_t[:, :], ps_t, ACT.Square).then_inc(zt_split, 1)
                    act.wait_ge(q_psum, c + 2)
                    nc.scalar.activation(cols(z_norm, c), ps_q, ACT.Copy, scale=-0.5).then_inc(q_split, 1)

            act.wait_ge(q_done, CHUNKS + 1)
            act.drain()
            act.sem_inc(pair_free, PAIRS)

            def similarities(i, last):
                act.wait_ge(dist_ready, i + 1)
                nc.scalar.activation(tiles(sim, i), dist[:, :, :], ACT.Exp, scale=-0.5).then_inc(sim_ready, 1)

            def rows_of(i, before):
                for k in range(K):
                    act.wait_ge(row_free, i * K + (k + 1))
                    for half_row in range(2):
                        for q in range(half_row * PAIRS // 2, (half_row + 1) * PAIRS // 2):
                            wait_apart(act, pair_ready, (i * K + k) * PAIRS + (q + 1))
                            nc.scalar.activation(rows[:, k % 2, q * 2 * CHUNK:(q + 1) * 2 * CHUNK],
                                                 psum[:, 2 * q:2 * q + 2, :].rearrange("p b n -> p (b n)"),
                                                 ACT.Relu, scale=-2.0, bias=tile_at(sq_col, i * K + k)).then_inc(pair_free, 1)
                        act.drain()
                        part = rows[:, k % 2, half_row * N // 2:(half_row + 1) * N // 2]
                        last = nc.scalar.activation(part, part, ACT.Copy, scale=-1.0)
                    last.then_inc(row_ready, 1)
                    if k == 1 and before:
                        similarities(i - 1, False)

            rows_of(0, False)
            with act.Fori(1, GROUPS) as i:
                rows_of(i, True)
            similarities(GROUPS - 1, True)

            with act.Fori(0, CHUNKS // 2) as i:
                for par in range(2):
                    c = i * 2 + par
                    product(2, c, par, prod_ready, c + 2)
                    act.wait_ge(w_used, c + 2 * CHUNKS + 2)
                    act.dma_start(tiles_of(out_tiles, c), out_sb[:, par]).then_inc(stored[par], DMA)
            for par in range(2):
                act.wait_ge(stored[par], (CHUNKS // 2 + 1) * DMA)

        @block.vector
        def _(dve):
            free_at_first(dve, w_used, z_done, q_done)

            dve.wait_ge(x_in, GROUPS * DMA)
            for t in range(TILES):
                nc.vector.bn_stats(stats[:, t, :], x_sb[:, t, :])
            dve.drain()
            for t in range(TILES):
                nc.vector.bn_aggr(mean_var[:, t, :], stats[:, t, :])
            dve.drain()
            nc.vector.tensor_scalar(var_eps[:, :], mean_var[:, :, 1], LN_EPS, None, ALU.add).then_inc(var_ready, 1)
            dve.wait_ge(small_in[0], DMA)
            nc.vector.tensor_scalar(beta[:, :], alpha[:, :], -1.0, 1.0, ALU.mult, ALU.add)
            dve.wait_ge(rstd_ready, 1)
            for t in range(TILES):
                last = nc.vector.tensor_scalar(h1[:, t, :], x_sb[:, t, :], mean_var[:, t, 0:1], rstd0[:, t:t + 1],
                                               ALU.subtract, ALU.mult)
                if t % K == K - 1:
                    last.then_inc(h_norm, 1)

            def row_sums(c, g):
                dve.drain()
                arrived(dve, 0, c, g)
                a = acc[:, :, :].rearrange("p k n -> p (k n)")
                r = ring[:, g % SLOTS].rearrange("p k n -> p (k n)")
                if g == 0:
                    nc.vector.tensor_copy(a, r).then_inc(dve_groups, 1)
                else:
                    nc.vector.tensor_tensor(a, a, r, ALU.add).then_inc(dve_groups, 1)

            def fold_sums():
                dve.drain()
                nc.vector.tensor_tensor(acc[:, 0:2, :], acc[:, 0:2, :], acc[:, 2:4, :], ALU.add)
                dve.drain()
                nc.vector.tensor_tensor(deg_part[:, :], acc[:, 0, :], acc[:, 1, :], ALU.add)

            def mix(c, par):
                dve.wait_ge(pe_groups, (c + 1) * GROUPS)
                nc.vector.scalar_tensor_tensor(out=prod_t[:, :], in0=psum[:, par, :], scalar=alpha[:, 0:1], in1=cols(h_t, c),
                                               op0=ALU.mult, op1=ALU.add).then_inc(y1_ready, 1)

            def finish1_a(c):
                dve.wait_ge(w_ready, c + 1)
                nc.vector.tensor_copy(tiles(deg, c), ps_deg)
                nc.vector.tensor_copy(pow_in[:, 1, :], ps_deg)
                nc.vector.tensor_scalar(out_deg[:, :], ps_deg, alpha[:, 0:1], beta[:, 0:1], ALU.mult, ALU.add)
                dve.drain()
                nc.vector.tensor_scalar(deg_zero[:, :], out_deg[:, :], 0.0, None, ALU.is_equal)
                dve.drain()
                nc.vector.tensor_tensor(deg_safe[:, :], out_deg[:, :], deg_zero[:, :], ALU.add)
                dve.drain()
                nc.vector.reciprocal(inv_deg[:, :], deg_safe[:, :])
                nc.vector.tensor_scalar(deg_zero[:, :], deg_zero[:, :], -1.0, 1.0, ALU.mult, ALU.add)
                dve.drain()
                nc.vector.tensor_tensor(inv_deg[:, :], inv_deg[:, :], deg_zero[:, :], ALU.mult)
                dve.drain()
                nc.vector.tensor_tensor(work[:, :, :], ps_w, over_features(inv_deg[:, :]), ALU.mult).then_inc(w_used, 1)
                dve.drain()
                nc.vector.tensor_tensor(work[:, :, :], work[:, :, :], over_tiles(b_row[:, :]), ALU.add)
                dve.drain()
                nc.vector.scalar_tensor_tensor(out=tiles(x_sb, c), in0=work[:, :, :], scalar=0.0, in1=tiles(x_sb, c),
                                               op0=ALU.max, op1=ALU.add)
                dve.drain()
                for k in range(K):
                    nc.vector.bn_stats(stats[:, k, :], tile_at(x_sb, c * K + k)[:, 0])
                dve.drain()
                for k in range(K):
                    nc.vector.bn_aggr(mean_var[:, k, :], stats[:, k, :])
                dve.drain()
                dve.wait_ge(h1_ready, c + 1)
                nc.vector.tensor_scalar(pow_in[:, 0, :], mean_var[:, 0:K, 1], LN_EPS, None, ALU.add).then_inc(pow_wanted, 1)

            def finish1_b(c):
                dve.wait_ge(pow_ready, c + 1)
                for k in range(K):
                    last = nc.vector.tensor_scalar(norm[:, k, :], tile_at(x_sb, c * K + k)[:, 0], mean_var[:, k, 0:1],
                                                   pow_out[:, 0, k:k + 1], ALU.subtract, ALU.mult)
                last.then_inc(norm_ready, 1)

            dve.wait_ge(small_in[5], DMA)

            def sums_of(c, before, par=None):
                if before is not None:
                    mix(before, par)
                for g in range(GROUPS):
                    row_sums(c, g)
                    if before is not None and g == 1:
                        finish1_a(before)
                    if before is not None and g == 2:
                        finish1_b(before)
                fold_sums()

            sums_of(0, None)
            dve.wait_ge(ht_ready, GROUPS)
            with dve.Fori(0, CHUNKS // 2 - 1) as i:
                sums_of(i * 2 + 1, i * 2, 0)
                sums_of(i * 2 + 2, i * 2 + 1, 1)
            sums_of(CHUNKS - 1, CHUNKS - 2, 0)
            mix(CHUNKS - 1, 1)
            finish1_a(CHUNKS - 1)
            finish1_b(CHUNKS - 1)

            dve.wait_ge(small_in[6], DMA)
            with dve.Fori(0, CHUNKS) as c:
                dve.wait_ge(w_ready, c + CHUNKS + 1)
                for k in range(K):
                    last = nc.vector.scalar_tensor_tensor(out=work[:, k, :], in0=ps_w[:, k, :], scalar=tile_at(d_col, c * K + k),
                                                          in1=b1_row[:, :], op0=ALU.mult, op1=ALU.add)
                last.then_inc(w_used, 1)
                dve.drain()
                dve.wait_ge(h1_ready, CHUNKS + 1)
                dve.wait_ge(zt_psum, c + 1)
                dve.wait_ge(sq_ready, c + 1)
                nc.vector.scalar_tensor_tensor(out=norm[:, :, :], in0=work[:, :, :], scalar=LEAK, in1=work[:, :, :],
                                               op0=ALU.mult, op1=ALU.max).then_inc(z_ready, 1)
                dve.wait_ge(zt_split, c + 1)
                nc.vector.tensor_tensor(cols(z_lo, c), ps_t, cols(z_hi, c).bitcast(F32), ALU.subtract).then_inc(z_done, 1)
                dve.wait_ge(q_split, c + 1)
                lower = cols(z_norm, c)[P // 2:P]
                nc.vector.scalar_tensor_tensor(out=lower, in0=ps_q[P // 2:P], scalar=-0.5, in1=lower.bitcast(F32),
                                               op0=ALU.mult, op1=ALU.subtract).then_inc(q_done, 1)

            dve.sem_inc(row_free, 2)

            def search(i, before):
                dve.drain()
                for k in range(K):
                    wait_apart(dve, row_ready, i * K + (k + 1))
                    nc.vector.max(top8[:, k, :], rows[:, k % 2, :])
                    dve.drain()
                    nc.vector.max_index(idx8[:, k, :], top8[:, k, :], rows[:, k % 2, :]).then_inc(row_free, 1)
                    if k == 2 and before:
                        degrees(i - 1)
                dve.drain()
                nc.vector.tensor_copy(tiles(near, i), idx8[:, :, 0:NEAR])
                nc.vector.tensor_scalar(dist_in[:, :, :], top8[:, :, 0:NEAR], -1.0, SIM_EPS, ALU.mult, ALU.add).then_inc(dist_wanted, 1)

            def degrees(i):
                dve.wait_ge(sim_ready, i + 1)
                nc.vector.tensor_reduce(sim_sum[:, :], tiles(sim, i), AX.X, ALU.add)
                dve.drain()
                nc.vector.tensor_tensor(sim_deg[:, :], sim_sum[:, :], tiles(deg, i), ALU.add).then_inc(deg2_wanted, 1)

            search(0, False)
            with dve.Fori(1, GROUPS) as i:
                search(i, True)
            degrees(GROUPS - 1)

            def lay_indices(c, par):
                nc.vector.tensor_copy(idx_now[:, par, :].rearrange("p (k j) -> p k j", k=K), tiles(near, c)).then_inc(idx_ready, 1)

            def near_sums(i, c, par):
                dve.wait_ge(rows_in[par], (i + 1) * (K * NEAR * DMA))
                dve.wait_ge(prod_ready, c + 1)
                for j in range(NEAR):
                    for k in range(K):
                        s = tile_at(sim, c * K + k)[:, 0, j:j + 1]
                        row = gathered[:, par, k * NEAR + j, :]
                        if j == 0:
                            last = nc.vector.tensor_scalar(near_sum[:, k, :], row, s, None, ALU.mult)
                        else:
                            last = nc.vector.scalar_tensor_tensor(out=near_sum[:, k, :], in0=row, scalar=s, in1=near_sum[:, k, :],
                                                                  op0=ALU.mult, op1=ALU.add)
                    if j < NEAR - 1:
                        dve.drain()
                last.then_inc(near_ready, 1)
                nc.vector.tensor_tensor(x1_b2[:, :, :], tiles(x_sb, c), over_tiles(b2_row[:, :]), ALU.add)

            def outputs(i, c, par):
                dve.drain()
                dve.wait_ge(w_ready, c + 2 * CHUNKS + 1)
                dve.wait_ge(stored[par], (i + 1) * DMA)
                for k in range(K):
                    last = nc.vector.scalar_tensor_tensor(out=out_sb[:, par, k, :], in0=ps_w[:, k, :], scalar=tile_at(d2_col, c * K + k),
                                                          in1=x1_b2[:, k, :], op0=ALU.mult, op1=ALU.add)
                last.then_inc(w_used, 1)

            dve.wait_ge(small_in[7], DMA)
            dve.drain()
            for par in range(2):
                lay_indices(par, par)
            with dve.Fori(0, CHUNKS // 2 - 1) as i:
                for par in range(2):
                    near_sums(i, i * 2 + par, par)
                    lay_indices(i * 2 + (par + 2), par)
                    outputs(i, i * 2 + par, par)
            for par in range(2):
                near_sums(CHUNKS // 2 - 1, CHUNKS - 2 + par, par)
                outputs(CHUNKS // 2 - 1, CHUNKS - 2 + par, par)

        @block.gpsimd
        def _(pool):
            nc.gpsimd.memset(neg_half[:, :], -0.5)
            nc.gpsimd.memset(half[:, :, :], 0.5)
            nc.gpsimd.memset(pick[:, :].bitcast(F32), 0.0)
            pool.drain()
            nc.gpsimd.memset(pick[0:1, :].bitcast(F32), 1.0)
            pool.drain()
            nc.gpsimd.memset(pick[P // 2:P // 2 + 1, :].bitcast(F32), 1.0)
            pool.drain()
            nc.gpsimd.memset(ones[:, :], 1.0).then_inc(consts, 1)

            pool.wait_ge(var_ready, 1)
            nc.gpsimd.tensor_tensor(rstd0[:, :], var_eps[:, :], neg_half[:, :], ALU.pow).then_inc(rstd_ready, 1)

            with pool.Fori(0, CHUNKS) as c:
                pool.wait_ge(pow_wanted, c + 1)
                nc.gpsimd.tensor_tensor(pow_out[:, :, :], pow_in[:, :, :],
                                        neg_half[:, 0:2 * K].rearrange("p (a k) -> p a k", a=2), ALU.pow).then_inc(pow_ready, 1)

            def stage(i, k):
                at = (bass.ds((i * K + k) * P, P) if not isinstance(i, int) else slice((i * K + k) * P, (i * K + k + 1) * P))
                nc.gpsimd.tensor_copy(z_hi_now[:, k, :], z_hi[:, at].bitcast(F32))
                nc.gpsimd.tensor_copy(z_lo_now[:, k, :], z_lo[:, at].bitcast(F32)).then_inc(z_staged, 1)

            def scaled(i):
                pool.wait_ge(dist_wanted, i + 1)
                nc.gpsimd.tensor_tensor(dist[:, :, :], dist_in[:, :, :], half[:, :, :], ALU.pow).then_inc(dist_ready, 1)
                pool.wait_ge(deg2_wanted, i + 1)
                nc.gpsimd.tensor_tensor(tiles(d2_col, i), sim_deg[:, :], neg_half[:, 0:K], ALU.pow)
                pool.drain()
                nc.gpsimd.tensor_tensor(tiles(feat_a, i), tiles(h1, i), tiles(d2_col, i).unsqueeze(2).to_broadcast([P, K, P]),
                                        ALU.mult).then_inc(feat_ready, 1)
                pool.wait_ge(feat_ready, i + 1)
                pool.dma_start(tiles_of(u_tiles, i), tiles(feat_a, i)).then_inc(u_stored, DMA)

            pool.wait_ge(z_done, CHUNKS + 1)
            for k in range(K):
                stage(0, k)
            with pool.Fori(0, GROUPS - 1) as i:
                for k in range(K):
                    pool.wait_ge(pair_ready, (i * K + k + 1) * PAIRS)
                    stage(i + 1, k)
                scaled(i)
            scaled(GROUPS - 1)

            pool.wait_ge(u_stored, GROUPS * DMA)
            with pool.Fori(0, CHUNKS // 2) as i:
                for par in range(2):
                    wait_apart(pool, idx_ready, i * 2 + (par + 1))
                    for m in range(K * NEAR):
                        nc.gpsimd.indirect_dma_start(
                            out=gathered[:, par, m, :], out_offset=None, in_=u_d,
                            in_offset=bass.IndirectOffsetOnAxis(ap=idx_now[:, par, m:m + 1], axis=0)).then_inc(rows_in[par], DMA)


def kernel(x, adj, L0_gnn_t, L0_gnn_alpha, L0_gnn_W, L0_gnn_b, L1_gnn_W1, L1_gnn_b1, L1_gnn_W2, L1_gnn_b2):
    import numpy as np
    import concourse.bacc as bacc
    from concourse.bass_utils import run_bass_kernel_spmd

    n, h = x.shape
    blocks = np.asarray(adj).T.reshape(n // CHUNK, K, P, n // CHUNK, CHUNK).transpose(3, 0, 2, 1, 4)
    arrays = {
        "x": np.ascontiguousarray(x),
        "at": np.ascontiguousarray(blocks).reshape(n // CHUNK, n // CHUNK, P, K * CHUNK),
        "alpha": np.ascontiguousarray(np.broadcast_to(np.asarray(L0_gnn_alpha).reshape(1, 1), (P, 1))),
        "wt": np.ascontiguousarray(np.asarray(L0_gnn_W).T),
        "b": np.ascontiguousarray(np.broadcast_to(np.asarray(L0_gnn_b), (P, h))),
        "w1": np.ascontiguousarray(L1_gnn_W1),
        "b1": np.ascontiguousarray(np.broadcast_to(np.asarray(L1_gnn_b1), (P, h))),
        "w2": np.ascontiguousarray(L1_gnn_W2),
        "b2": np.ascontiguousarray(np.broadcast_to(np.asarray(L1_gnn_b2), (P, h))),
        "ident": np.eye(P, dtype=np.float32),
    }
    nc = bacc.Bacc("TRN2", target_bir_lowering=False, num_devices=1)
    ins = [nc.dram_tensor(f"in_{k}", a.shape, mybir.dt.from_np(a.dtype), kind="ExternalInput").ap() for k, a in arrays.items()]
    out = nc.dram_tensor("out", (n, h), F32, kind="ExternalOutput").ap()
    scratch = nc.dram_tensor("scaled_features", (n, h), F32, kind="Internal").ap()
    graph_layers(nc, *ins, out, scratch)
    r = run_bass_kernel_spmd(nc, [{f"in_{k}": a for k, a in arrays.items()}], core_ids=[0])
    return r.results[0]["out"]
```

```python
from contextlib import ExitStack

import concourse.bass as bass
from concourse import mybir

F32 = mybir.dt.float32
F32R = mybir.dt.float32r
U32 = mybir.dt.uint32
ALU = mybir.AluOpType
ACT = mybir.ActivationFunctionType
AX = mybir.AxisListType

P = 128
CHUNK = 512
K = CHUNK // P
SLOTS = 4
NEAR = 4
TOP = 8
LN_EPS = 1e-5
SIM_EPS = 1e-10
LEAK = 0.1
DMA = 16


def graph_layers(nc, x_d, at_d, alpha_d, wt_d, b_d, w1_d, b1_d, w2_d, b2_d, ident_d, out_d, u_d):
    N, H = x_d.shape
    TILES = N // P
    CHUNKS = N // CHUNK
    GROUPS = TILES // K
    LAPS = GROUPS // SLOTS
    SWEEP = CHUNKS * GROUPS
    PAIRS = CHUNKS // 2
    assert H == P and CHUNKS % 2 == 0 and GROUPS == LAPS * SLOTS and PAIRS * 2 == 8

    x_tiles = x_d.rearrange("(t p) f -> p t f", p=P)
    out_tiles = out_d.rearrange("(t p) f -> p t f", p=P)
    u_tiles = u_d.rearrange("(t p) f -> p t f", p=P)

    with ExitStack() as ctx:
        def sb(name, shape, dt=F32):
            return ctx.enter_context(nc.sbuf_tensor(name, shape, dt))

        def sem(name):
            return ctx.enter_context(nc.semaphore(name))

        x_sb = sb("x_sb", [P, TILES, P])
        h1 = sb("h1", [P, TILES, P])
        ring = sb("ring", [P, SLOTS, K, CHUNK])
        ident = sb("ident", [P, P])
        ones = sb("ones", [P, P])
        zeros = sb("zeros", [P, CHUNK])
        wt = sb("wt", [P, P])
        w1 = sb("w1", [P, P])
        w2 = sb("w2", [P, P])
        b_row = sb("b_row", [P, P])
        b1_row = sb("b1_row", [P, P])
        b2_row = sb("b2_row", [P, P])
        alpha = sb("alpha", [P, 1])
        beta = sb("beta", [P, 1])
        neg_half = sb("neg_half", [P, TILES])
        half = sb("half", [P, K, NEAR])
        stats = sb("stats", [P, TILES, 6])
        mean_var = sb("mean_var", [P, TILES, 2])
        var_eps = sb("var_eps", [P, TILES])
        rstd0 = sb("rstd0", [P, TILES])
        deg = sb("deg", [P, TILES])
        d_col = sb("d_col", [P, TILES])
        d2_col = sb("d2_col", [P, TILES])
        sq_col = sb("sq_col", [P, TILES])
        sim = sb("sim", [P, TILES, NEAR])
        near = sb("near", [P, TILES, NEAR], U32)
        pow_in = sb("pow_in", [P, 2, K])
        pow_out = sb("pow_out", [P, 2, K])
        out_deg = sb("out_deg", [P, K])
        deg_zero = sb("deg_zero", [P, K])
        deg_safe = sb("deg_safe", [P, K])
        inv_deg = sb("inv_deg", [P, K])
        prod_t = sb("prod_t", [P, CHUNK])
        deg_part = sb("deg_part", [P, CHUNK])
        work = sb("work", [P, K, P])
        norm = sb("norm", [P, K, P])
        square = sb("square", [P, K, P])
        z_sq_t = sb("z_sq_t", [P, CHUNK])
        feat_now = sb("feat_now", [P, K, P])
        z_hi_now = sb("z_hi_now", [P, K, P], F32R)
        z_lo_now = sb("z_lo_now", [P, K, P], F32R)
        pick = sb("pick", [P, P], F32R)
        top8 = sb("top8", [P, K, TOP])
        idx8 = sb("idx8", [P, K, TOP], U32)
        dist_in = sb("dist_in", [P, K, NEAR])
        dist = sb("dist", [P, K, NEAR])
        sim_sum = sb("sim_sum", [P, K])
        sim_deg = sb("sim_deg", [P, K])
        idx_now = sb("idx_now", [P, 2, K * NEAR], U32)

        KB = 1024
        arena = sb("arena", [P, 112 * KB // 4])
        arena_at = nc.sbuf_base - 112 * KB

        def region(name, offset, shape, dt=F32):
            return nc.alloc_sbuf_tensor_at(name, shape, dt, offset=arena_at + offset * KB)

        h_t = region("h_t", 32, [P, N])
        acc = region("acc", 48, [P, K, CHUNK])
        feat_a = region("feat_a", 64, [P, TILES, P])
        feat_b = [region(f"feat_b_{x}", o, [P, TILES, P], F32R) for x, o in (("hi", 0), ("lo", 16))]
        a_parts2 = [region(f"a2_{x}", o, [P, 2, K, CHUNK], F32R) for x, o in (("hi", 80), ("lo", 96))]
        z_hi = region("z_hi", 32, [P, N], F32R)
        z_lo = region("z_lo", 48, [P, N], F32R)
        z_norm = region("z_norm", 64, [P, N], F32R)
        rows = region("rows", 0, [P, 2, N])
        feat_c = [region(f"feat_c_{x}", o, [P, TILES, P], F32R) for x, o in (("hi", 80), ("lo", 96))]
        a_parts3 = [region(f"a3_{x}", o, [P, 2, K, CHUNK], F32R) for x, o in (("hi", 0), ("lo", 16))]
        gathered = region("gathered", 32, [P, 2, K * NEAR, P])
        y_all = region("y_all", 48, [P, N])
        near_sum = region("near_sum", 64, [P, K, P])
        out_sb = region("out_sb", 68, [P, 2, K, P])

        psum = ctx.enter_context(nc.psum_tensor("psum", [P, 8, CHUNK], F32))
        BANK_W, BANK_DEG, BANK_T, BANK_Q = 2, 3, 4, 5
        BANK_PAIRS = 4
        ps_w = psum[:, BANK_W, :].rearrange("p (k f) -> p k f", k=K)
        ps_deg = psum[:, BANK_DEG, 0:K]
        ps_t = psum[:, BANK_T, :]
        ps_q = psum[:, BANK_Q, :]

        x_in = sem("x_in")
        small_in = [sem(f"small_in{i}") for i in range(8)]
        load_done = [sem(f"load_done{s}") for s in range(SLOTS)]
        pe_groups = sem("pe_groups")
        dve_groups = sem("dve_groups")
        hi_ready = sem("hi_ready")
        tile_in = [sem(f"tile_in{k}") for k in range(K)]
        tile_used = sem("tile_used")
        unread = sem("unread")
        consts = sem("consts")
        var_ready = sem("var_ready")
        rstd_ready = sem("rstd_ready")
        h_norm = sem("h_norm")
        h_ready = sem("h_ready")
        ht_psum = sem("ht_psum")
        ht_ready = sem("ht_ready")
        y1_ready = sem("y1_ready")
        y_ready = sem("y_ready")
        y_kept = sem("y_kept")
        near_psum = sem("near_psum")
        y3_ready = sem("y3_ready")
        w_ready = sem("w_ready")
        w_used = sem("w_used")
        pow_wanted = sem("pow_wanted")
        pow_ready = sem("pow_ready")
        norm_ready = sem("norm_ready")
        h1_ready = sem("h1_ready")
        feat_b_ready = sem("feat_b_ready")
        z_ready = sem("z_ready")
        sq_ready = sem("sq_ready")
        zt_psum = sem("zt_psum")
        zt_split = sem("zt_split")
        z_done = sem("z_done")
        q_psum = sem("q_psum")
        q_split = sem("q_split")
        q_done = sem("q_done")
        z_staged = sem("z_staged")
        pair_ready = sem("pair_ready")
        pair_free = sem("pair_free")
        row_ready = sem("row_ready")
        row_free = sem("row_free")
        dist_wanted = sem("dist_wanted")
        dist_ready = sem("dist_ready")
        sim_ready = sem("sim_ready")
        deg2_wanted = sem("deg2_wanted")
        feat_ready = sem("feat_ready")
        feat_c_ready = sem("feat_c_ready")
        u_stored = sem("u_stored")
        idx_ready = sem("idx_ready")
        rows_in = [[sem(f"rows_in{s}_{k}") for k in range(K)] for s in range(2)]
        rows_scaled = sem("rows_scaled")
        near_ready = sem("near_ready")
        b2_added = sem("b2_added")
        stored = [sem(f"stored{s}") for s in range(2)]

        def free_at_first(eng, *whats):
            for what in whats:
                eng.sem_inc(what, 1)

        EARLY = 2
        NEAR_AT = 4
        at_tiles = at_d.rearrange("c g p (k n) -> g k p c n", k=K)

        def tiles(t, c):
            return t[:, bass.ds(c * K, K)] if not isinstance(c, int) else t[:, c * K:(c + 1) * K]

        def tile_at(t, i):
            return t[:, bass.ds(i, 1)] if not isinstance(i, int) else t[:, i:i + 1]

        def cols(t, c):
            return t[:, bass.ds(c * CHUNK, CHUNK)] if not isinstance(c, int) else t[:, c * CHUNK:(c + 1) * CHUNK]

        def over_features(v):
            return v.unsqueeze(2).to_broadcast([P, K, P])

        def over_tiles(v):
            return v.unsqueeze(1).to_broadcast([P, K, P])

        def wait_apart(eng, what, value):
            eng.wait_ge(what, value)
            eng.sem_inc(unread, 1)

        def tiles_of(d, c):
            return tiles(d, c)

        def early_tile(k):
            return ring[:, SLOTS // 2 + k // 2, (k % 2) * EARLY:(k % 2 + 1) * EARLY, :]

        def arrived(eng, sweep, c, g):
            before = sweep * CHUNKS * LAPS - (EARLY * LAPS if sweep == 2 else 0)
            eng.wait_ge(load_done[g % SLOTS], (c * LAPS + (g // SLOTS + 1 + before)) * DMA)

        def split_count(sweep, c, g):
            return c * GROUPS + (g + 1 + ((sweep - 1) * SWEEP - (EARLY * GROUPS if sweep == 2 else 0)))

        block = ctx.enter_context(nc.Block())

        @block.sync
        def _(sp):
            for g in range(GROUPS):
                sp.dma_start(x_sb[:, g * K:(g + 1) * K, :], x_tiles[:, g * K:(g + 1) * K, :]).then_inc(x_in, DMA)

            def load(sweep, c, g):
                n = c * GROUPS + g + (sweep * SWEEP - (EARLY * GROUPS if sweep == 2 else 0))
                if sweep == 0 and (not isinstance(n, int) or n >= SLOTS):
                    sp.wait_ge(pe_groups, n - SLOTS + 1)
                if sweep == 1 and isinstance(n, int) and n - SLOTS < SWEEP:
                    sp.wait_ge(pe_groups, n - SLOTS + 1)
                if not isinstance(n, int) or n >= SLOTS:
                    sp.wait_ge(dve_groups, n - SLOTS + 1)
                sp.dma_start(ring[:, g % SLOTS].rearrange("p k n -> p (k n)"),
                             at_d[c, g]).then_inc(load_done[g % SLOTS], DMA)

            for sweep in range(2):
                for g in range(GROUPS):
                    load(sweep, 0, g)
                with sp.Fori(1, CHUNKS) as c:
                    for g in range(GROUPS):
                        load(sweep, c, g)

            def load_tiles(i, first):
                for k in range(K):
                    if not first:
                        sp.wait_ge(tile_used, i * K + k + 1 - K)
                    sp.dma_start(early_tile(k), at_tiles[i, k][:, 0:EARLY, :]).then_inc(tile_in[k], DMA)

            sp.wait_ge(dve_groups, 2 * SWEEP)
            load_tiles(0, True)
            with sp.Fori(1, GROUPS) as i:
                load_tiles(i, False)
            for g in range(GROUPS):
                if g % SLOTS == SLOTS // 2 and g < SLOTS:
                    sp.wait_ge(tile_used, TILES)
                load(2, EARLY, g)
            with sp.Fori(EARLY + 1, CHUNKS) as c:
                for g in range(GROUPS):
                    load(2, c, g)

        @block.tensor
        def _(pe):
            def transposes(g):
                pe.wait_ge(h_ready, g + 1)
                if g >= 2:
                    pe.wait_ge(ht_ready, g - 1)
                for k in range(K):
                    last = nc.tensor.transpose(psum[:, BANK_T + g % 2, k * P:(k + 1) * P], feat_a[:, g * K + k, :], ident[:, :])
                last.then_inc(ht_psum, 1)

            def stream(sweep, c, par, feat, between):
                first = isinstance(c, int) and c == 0
                for g in range(GROUPS):
                    if sweep == 0 and first:
                        transposes(g)
                    arrived(pe, sweep, c, g)
                    for k in range(K):
                        t = g * K + k
                        last = nc.tensor.matmul(psum[:, par, :], feat[:, t, :], ring[:, g % SLOTS, k, :],
                                                start=(t == 0), stop=(t == TILES - 1))
                    last.then_inc(pe_groups, 1)
                    if between is not None:
                        between(g)

            def stream_parts(sweep, c, par, feat, a_parts, between):
                for g in range(GROUPS):
                    if sweep == 1 and isinstance(c, int) and c == 0:
                        pe.wait_ge(feat_b_ready, g + 2)
                    if sweep == 2 and g == 0:
                        pe.wait_ge(y_kept, c - 1)
                    if sweep == 2 and isinstance(c, int) and c == EARLY:
                        pe.wait_ge(feat_c_ready, g + 1)
                    pe.wait_ge(hi_ready, split_count(sweep, c, g))
                    for k in range(K):
                        for m in range(2):
                            nc.tensor.matmul(psum[:, par, :], feat[m][:, g * K + k, :], a_parts[0][:, g % 2, k, :],
                                             start=(g == k == m == 0), stop=False)
                    pe.wait_ge(dve_groups, split_count(sweep, c, g) + SWEEP)
                    for k in range(K):
                        last = nc.tensor.matmul(psum[:, par, :], feat[0][:, g * K + k, :], a_parts[1][:, g % 2, k, :],
                                                start=False, stop=(g == GROUPS - 1 and k == K - 1))
                    last.then_inc(pe_groups, 1)
                    if between is not None:
                        between(g)

            def weights(n, rhs):
                pe.wait_ge(w_used, n + 1)
                for k in range(K):
                    last = nc.tensor.matmul(ps_w[:, k, :], prod_t[:, k * P:(k + 1) * P], rhs[:, :], start=True, stop=True)
                return last

            def finish1(c, g):
                if g == 1:
                    pe.wait_ge(y1_ready, c + 1)
                    weights(c, wt)
                    for k in range(K):
                        last = nc.tensor.matmul(ps_deg[:, k:k + 1], deg_part[:, k * P:(k + 1) * P], ones[:, 0:1], start=True, stop=True)
                    last.then_inc(w_ready, 1)

            def finish2(c, g):
                if g == 0:
                    pe.wait_ge(y_ready, c + 1)
                    weights(c + CHUNKS, w1).then_inc(w_ready, 1)
                if g == 3:
                    pe.wait_ge(z_ready, c + 1)
                    pe.wait_ge(z_done, c + 1)
                    for k in range(K):
                        last = nc.tensor.transpose(ps_t[:, k * P:(k + 1) * P], norm[:, k, :], ident[:, :])
                    last.then_inc(zt_psum, 1)
                if g == 5:
                    pe.wait_ge(zt_split, c + 1)
                    pe.wait_ge(q_done, c + 1)
                    nc.tensor.matmul(ps_q, ones[:, :], z_sq_t[:, :], start=True, stop=True).then_inc(q_psum, 1)

            def turn_near(c):
                pe.wait_ge(near_ready, c + 1)
                pe.wait_ge(y3_ready, c + 1)
                for k in range(K):
                    last = nc.tensor.transpose(ps_t[:, k * P:(k + 1) * P], near_sum[:, k, :], ident[:, :])
                last.then_inc(near_psum, 1)

            def weigh3(c):
                pe.wait_ge(y3_ready, c + 2)
                weights(c + 2 * CHUNKS, w2).then_inc(w_ready, 1)

            def finish3(c, g, near_at):
                if g == 2:
                    weigh3(c - 3)
                if g == near_at:
                    turn_near(c - 2)

            def first3(g):
                if g == 0:
                    turn_near(0)
                finish3(3, g, GROUPS - 1)

            free_at_first(pe, zt_psum, q_psum, near_psum)

            def run_sweep(stream, before, finish):
                stream(0, 0, before)
                with pe.Fori(0, CHUNKS // 2 - 1) as i:
                    for j in range(1, 3):
                        stream(i * 2 + j, j % 2, lambda g, c=i * 2 + j: finish(c, g))
                stream(CHUNKS - 1, 1, lambda g: finish(CHUNKS - 1, g))

            for i in range(1, 8):
                pe.wait_ge(small_in[i], DMA)
            pe.wait_ge(consts, 1)
            run_sweep(lambda c, par, b: stream(0, c, par, feat_a, b), None, lambda c, g: finish1(c - 1, g))
            run_sweep(lambda c, par, b: stream_parts(1, c, par, feat_b, a_parts2, b),
                      lambda g: finish1(CHUNKS - 1, g), lambda c, g: finish2(c - 1, g))
            for g in range(GROUPS):
                finish2(CHUNKS - 1, g)

            pe.wait_ge(z_done, CHUNKS + 1)
            pe.wait_ge(q_done, CHUNKS + 1)
            pe.wait_ge(w_used, 2 * CHUNKS + 1)
            for b in range(EARLY):
                nc.tensor.matmul(psum[:, b, :], zeros[:, 0:P], zeros[:, :], start=True, stop=False, skip_group_check=True)

            def early(i, k):
                pe.wait_ge(feat_ready, i + 1)
                pe.wait_ge(tile_in[k], (i + 1) * DMA)
                for b in range(EARLY):
                    last = nc.tensor.matmul(psum[:, b, :], feat_now[:, k, :], early_tile(k)[:, b, :],
                                            start=False, stop=False, skip_group_check=True)
                last.then_inc(tile_used, 1)

            def distances(i, lag):
                for k in range(K):
                    pe.wait_ge(z_staged, i * K + (k + 1))
                    for q in range(PAIRS):
                        pe.wait_ge(pair_free, (i * K + k) * PAIRS + (q + 1))
                        parts = ((pick[:, :], z_norm), (z_hi_now[:, k, :], z_hi), (z_hi_now[:, k, :], z_lo),
                                 (z_lo_now[:, k, :], z_hi))
                        for m, (lhs, rhs) in enumerate(parts):
                            for b in range(2):
                                last = nc.tensor.matmul(psum[:, BANK_PAIRS + 2 * (q % 2) + b, :], lhs, cols(rhs, 2 * q + b),
                                                        start=(m == 0), stop=(m == len(parts) - 1))
                        last.then_inc(pair_ready, 1)
                    if lag:
                        early(i - 2, k)

            for i in range(2):
                distances(i, False)
            with pe.Fori(2, GROUPS) as i:
                distances(i, True)
            for i in range(GROUPS - 2, GROUPS):
                for k in range(K):
                    early(i, k)
            pe.wait_ge(pair_free, TILES * PAIRS + 2)
            pe.wait_ge(y_kept, EARLY)

            stream_parts(2, EARLY, 0, feat_c, a_parts3, None)
            stream_parts(2, EARLY + 1, 1, feat_c, a_parts3, first3)
            with pe.Fori(EARLY // 2 + 1, CHUNKS // 2) as i:
                for par in range(2):
                    stream_parts(2, i * 2 + par, par, feat_c, a_parts3, lambda g, c=i * 2 + par: finish3(c, g, NEAR_AT + 1))
            weigh3(CHUNKS - 3)
            for c in range(CHUNKS - 2, CHUNKS):
                turn_near(c)
                weigh3(c)

        @block.scalar
        def _(act):
            for i, (to, of) in enumerate(((alpha, alpha_d), (ident, ident_d), (wt, wt_d), (w1, w1_d), (w2, w2_d),
                                          (b_row, b_d), (b1_row, b1_d), (b2_row, b2_d))):
                act.dma_start(to[:, :], of).then_inc(small_in[i], DMA)

            free_at_first(act, h1_ready, sq_ready)
            for par in range(2):
                act.sem_inc(stored[par], DMA)

            def h_of(g):
                act.wait_ge(h_norm, g + 1)
                nc.scalar.activation(feat_a[:, g * K:(g + 1) * K, :], h1[:, g * K:(g + 1) * K, :], ACT.Relu).then_inc(h_ready, 1)

            def ht_of(g):
                act.wait_ge(ht_psum, g + 1)
                nc.scalar.activation(cols(h_t, g), psum[:, BANK_T + g % 2, :], ACT.Copy, scale=beta[:, 0:1]).then_inc(ht_ready, 1)

            for g in range(GROUPS):
                h_of(g)
                if g >= 1:
                    ht_of(g - 1)
            ht_of(GROUPS - 1)

            def features(c):
                act.wait_ge(norm_ready, c + 1)
                nc.scalar.activation(tiles(h1, c), norm[:, :, :], ACT.Relu)
                nc.scalar.activation(tiles(d_col, c), pow_out[:, 1, :], ACT.Copy)
                act.wait_ge(feat_b_ready, c + 1)
                for k in range(K):
                    nc.scalar.activation(feat_now[:, k, :], norm[:, k, :], ACT.Relu, scale=pow_out[:, 1, k:k + 1])
                act.drain()
                nc.scalar.activation(tiles(feat_b[0], c), feat_now[:, :, :], ACT.Copy).then_inc(h1_ready, 1)

            with act.Fori(0, CHUNKS - 1) as c:
                features(c)

            def upper(sweep, c, g, a_parts):
                act.wait_ge(pe_groups, split_count(sweep, c, g) + (SWEEP - 2))
                arrived(act, sweep, c, g)
                nc.scalar.activation(a_parts[0][:, g % 2], ring[:, g % SLOTS], ACT.Copy).then_inc(hi_ready, 1)

            def finish2(c, par, g):
                if g == 1:
                    act.wait_ge(pe_groups, c * GROUPS + (SWEEP + GROUPS))
                    act.wait_ge(w_ready, c + CHUNKS)
                    nc.scalar.activation(prod_t[:, :], psum[:, par, :], ACT.Copy).then_inc(y_ready, 1)
                if g == 4:
                    act.drain()
                    wait_apart(act, z_ready, c + 1)
                    for k in range(K):
                        last = nc.scalar.activation(square[:, k, :], norm[:, k, :], ACT.Square,
                                                    accum_out=tile_at(sq_col, c * K + k))
                    last.then_inc(sq_ready, 1)
                if g == 5:
                    act.wait_ge(zt_psum, c + 2)
                    act.wait_ge(q_psum, c + 1)
                    nc.scalar.activation(cols(z_hi, c), ps_t, ACT.Copy)
                    nc.scalar.activation(z_sq_t[:, :], ps_t, ACT.Square).then_inc(zt_split, 1)
                if g == 7:
                    act.wait_ge(q_psum, c + 2)
                    nc.scalar.activation(cols(z_norm, c), ps_q, ACT.Copy, scale=-0.5).then_inc(q_split, 1)

            def chunk2(c, before, par):
                for g in range(GROUPS):
                    upper(1, c, g, a_parts2)
                    if before is not None:
                        finish2(before, par, g)
                    elif g == 4:
                        features(CHUNKS - 1)

            chunk2(0, None, None)
            with act.Fori(0, CHUNKS // 2 - 1) as i:
                chunk2(i * 2 + 1, i * 2, 0)
                chunk2(i * 2 + 2, i * 2 + 1, 1)
            chunk2(CHUNKS - 1, CHUNKS - 2, 0)
            for g in range(GROUPS):
                finish2(CHUNKS - 1, 1, g)

            act.wait_ge(q_done, CHUNKS + 1)
            act.drain()
            act.sem_inc(pair_free, 2)

            def similarities(i, last):
                act.wait_ge(dist_ready, i + 1)
                nc.scalar.activation(tiles(sim, i), dist[:, :, :], ACT.Exp, scale=-0.5).then_inc(sim_ready, 1)

            def rows_of(i, before):
                for k in range(K):
                    act.wait_ge(row_free, i * K + (k + 1))
                    for half_row in range(2):
                        for q in range(half_row * PAIRS // 2, (half_row + 1) * PAIRS // 2):
                            wait_apart(act, pair_ready, (i * K + k) * PAIRS + (q + 1))
                            nc.scalar.activation(rows[:, k % 2, q * 2 * CHUNK:(q + 1) * 2 * CHUNK],
                                                 psum[:, BANK_PAIRS + 2 * (q % 2):BANK_PAIRS + 2 * (q % 2) + 2, :].rearrange("p b n -> p (b n)"),
                                                 ACT.Relu, scale=-2.0, bias=tile_at(sq_col, i * K + k)).then_inc(pair_free, 1)
                        act.drain()
                        part = rows[:, k % 2, half_row * N // 2:(half_row + 1) * N // 2]
                        last = nc.scalar.activation(part, part, ACT.Copy, scale=-1.0)
                    last.then_inc(row_ready, 1)
                    if k == 1 and before:
                        similarities(i - 1, False)

            rows_of(0, False)
            with act.Fori(1, GROUPS) as i:
                rows_of(i, True)
            similarities(GROUPS - 1, True)

            def keep(c, par):
                nc.scalar.activation(cols(y_all, c), psum[:, par, :], ACT.Copy).then_inc(y_kept, 1)

            def store_out(c, slot):
                act.wait_ge(w_used, c + (2 * CHUNKS + 2))
                act.dma_start(tiles_of(out_tiles, c), out_sb[:, slot]).then_inc(stored[slot], DMA)

            def scale_rows(c, par, uses, k):
                wait_apart(act, rows_in[par][k], uses * (NEAR * DMA) + NEAR * DMA)
                for j in range(NEAR):
                    row = gathered[:, par, k * NEAR + j, :]
                    last = nc.scalar.activation(row, row, ACT.Copy, scale=tile_at(sim, c * K + k)[:, 0, j:j + 1])
                last.then_inc(rows_scaled, 1)

            def chunk3(c, par, uses, before, store, slot, near_at):
                for g in range(GROUPS):
                    upper(2, c, g, a_parts3)
                    if g == 1 and before is not None:
                        act.wait_ge(pe_groups, split_count(2, c, g) + (SWEEP - 2))
                        keep(c - 1, before)
                    for k in range(K):
                        if g == min(near_at - 3 + k, near_at - 1):
                            scale_rows(c - EARLY, par, uses, k)
                    if g == GROUPS - 1 and store is not None:
                        store_out(store, slot)

            act.wait_ge(tile_used, TILES)
            act.wait_ge(row_free, TILES + 2)
            for b in range(EARLY):
                keep(b, b)
            chunk3(EARLY, 0, 0, None, None, None, GROUPS)
            chunk3(EARLY + 1, 1, 0, 0, 0, 0, GROUPS - 2)
            with act.Fori(EARLY // 2 + 1, CHUNKS // 2) as i:
                chunk3(i * 2, 0, i - 1, 1, i * 2 - 3, 1, NEAR_AT)
                chunk3(i * 2 + 1, 1, i - 1, 0, i * 2 - 2, 0, NEAR_AT)
            for k in range(K):
                scale_rows(CHUNKS - 2, 0, CHUNKS // 2 - 1, k)
            act.wait_ge(pe_groups, split_count(2, CHUNKS - 1, GROUPS - 1) + SWEEP)
            keep(CHUNKS - 1, 1)
            store_out(CHUNKS - 3, 1)
            for k in range(K):
                scale_rows(CHUNKS - 1, 1, CHUNKS // 2 - 1, k)
            for c in range(CHUNKS - 2, CHUNKS):
                store_out(c, c % 2)
            for slot in range(2):
                act.wait_ge(stored[slot], (CHUNKS // 2 + 1) * DMA)

        @block.vector
        def _(dve):
            free_at_first(dve, w_used, z_done, q_done, y3_ready, feat_b_ready)

            dve.wait_ge(x_in, GROUPS * DMA)
            for t in range(TILES):
                nc.vector.bn_stats(stats[:, t, :], x_sb[:, t, :])
            dve.drain()
            for t in range(TILES):
                nc.vector.bn_aggr(mean_var[:, t, :], stats[:, t, :])
            dve.drain()
            nc.vector.tensor_scalar(var_eps[:, :], mean_var[:, :, 1], LN_EPS, None, ALU.add).then_inc(var_ready, 1)
            dve.wait_ge(small_in[0], DMA)
            nc.vector.tensor_scalar(beta[:, :], alpha[:, :], -1.0, 1.0, ALU.mult, ALU.add)
            dve.wait_ge(rstd_ready, 1)
            for t in range(TILES):
                last = nc.vector.tensor_scalar(h1[:, t, :], x_sb[:, t, :], mean_var[:, t, 0:1], rstd0[:, t:t + 1],
                                               ALU.subtract, ALU.mult)
                if t % K == K - 1:
                    last.then_inc(h_norm, 1)

            def row_sums(c, g):
                dve.drain()
                arrived(dve, 0, c, g)
                a = acc[:, :, :].rearrange("p k n -> p (k n)")
                r = ring[:, g % SLOTS].rearrange("p k n -> p (k n)")
                if g == 0:
                    nc.vector.tensor_copy(a, r).then_inc(dve_groups, 1)
                else:
                    nc.vector.tensor_tensor(a, a, r, ALU.add).then_inc(dve_groups, 1)

            def fold_sums():
                dve.drain()
                nc.vector.tensor_tensor(acc[:, 0:2, :], acc[:, 0:2, :], acc[:, 2:4, :], ALU.add)
                dve.drain()
                nc.vector.tensor_tensor(deg_part[:, :], acc[:, 0, :], acc[:, 1, :], ALU.add)

            def mix(c, par):
                dve.wait_ge(pe_groups, (c + 1) * GROUPS)
                nc.vector.scalar_tensor_tensor(out=prod_t[:, :], in0=psum[:, par, :], scalar=alpha[:, 0:1], in1=cols(h_t, c),
                                               op0=ALU.mult, op1=ALU.add).then_inc(y1_ready, 1)

            def finish1_a(c):
                dve.wait_ge(w_ready, c + 1)
                nc.vector.tensor_copy(tiles(deg, c), ps_deg)
                nc.vector.tensor_copy(pow_in[:, 1, :], ps_deg)
                nc.vector.tensor_scalar(out_deg[:, :], ps_deg, alpha[:, 0:1], beta[:, 0:1], ALU.mult, ALU.add)
                dve.drain()
                nc.vector.tensor_scalar(deg_zero[:, :], out_deg[:, :], 0.0, None, ALU.is_equal)
                dve.drain()
                nc.vector.tensor_tensor(deg_safe[:, :], out_deg[:, :], deg_zero[:, :], ALU.add)
                dve.drain()
                nc.vector.reciprocal(inv_deg[:, :], deg_safe[:, :])
                nc.vector.tensor_scalar(deg_zero[:, :], deg_zero[:, :], -1.0, 1.0, ALU.mult, ALU.add)
                dve.drain()
                nc.vector.tensor_tensor(inv_deg[:, :], inv_deg[:, :], deg_zero[:, :], ALU.mult)
                dve.drain()
                nc.vector.tensor_tensor(work[:, :, :], ps_w, over_features(inv_deg[:, :]), ALU.mult).then_inc(w_used, 1)
                dve.drain()
                nc.vector.tensor_tensor(work[:, :, :], work[:, :, :], over_tiles(b_row[:, :]), ALU.add)
                dve.drain()
                nc.vector.scalar_tensor_tensor(out=tiles(x_sb, c), in0=work[:, :, :], scalar=0.0, in1=tiles(x_sb, c),
                                               op0=ALU.max, op1=ALU.add)
                dve.drain()
                for k in range(K):
                    nc.vector.bn_stats(stats[:, k, :], tile_at(x_sb, c * K + k)[:, 0])
                dve.drain()
                for k in range(K):
                    nc.vector.bn_aggr(mean_var[:, k, :], stats[:, k, :])
                dve.drain()
                dve.wait_ge(h1_ready, c + 1)
                nc.vector.tensor_scalar(pow_in[:, 0, :], mean_var[:, 0:K, 1], LN_EPS, None, ALU.add).then_inc(pow_wanted, 1)

            def finish1_b(c):
                dve.wait_ge(pow_ready, c + 1)
                for k in range(K):
                    last = nc.vector.tensor_scalar(norm[:, k, :], tile_at(x_sb, c * K + k)[:, 0], mean_var[:, k, 0:1],
                                                   pow_out[:, 0, k:k + 1], ALU.subtract, ALU.mult)
                last.then_inc(norm_ready, 1)

            def finish1_c(c):
                dve.wait_ge(h1_ready, c + 2)
                nc.vector.tensor_tensor(tiles(feat_b[1], c), feat_now[:, :, :], tiles(feat_b[0], c).bitcast(F32),
                                        ALU.subtract).then_inc(feat_b_ready, 1)

            dve.wait_ge(small_in[5], DMA)

            def sums_of(c, before, par=None):
                if before is not None:
                    mix(before, par)
                for g in range(GROUPS):
                    row_sums(c, g)
                    if before is not None and g == 1:
                        finish1_a(before)
                    if before is not None and g == 2:
                        finish1_b(before)
                    if before is not None and g == 4:
                        finish1_c(before)
                fold_sums()

            sums_of(0, None)
            dve.wait_ge(ht_ready, GROUPS)
            with dve.Fori(0, CHUNKS // 2 - 1) as i:
                sums_of(i * 2 + 1, i * 2, 0)
                sums_of(i * 2 + 2, i * 2 + 1, 1)
            sums_of(CHUNKS - 1, CHUNKS - 2, 0)
            mix(CHUNKS - 1, 1)

            def lower(sweep, c, g, a_parts):
                dve.wait_ge(hi_ready, split_count(sweep, c, g))
                nc.vector.tensor_tensor(a_parts[1][:, g % 2], ring[:, g % SLOTS], a_parts[0][:, g % 2].bitcast(F32),
                                        ALU.subtract).then_inc(dve_groups, 1)

            def finish2(c, g):
                if g == 2:
                    dve.drain()
                    dve.wait_ge(w_ready, c + (CHUNKS + 1))
                    for k in range(K):
                        last = nc.vector.scalar_tensor_tensor(out=work[:, k, :], in0=ps_w[:, k, :], scalar=tile_at(d_col, c * K + k),
                                                              in1=b1_row[:, :], op0=ALU.mult, op1=ALU.add)
                    last.then_inc(w_used, 1)
                    dve.drain()
                    dve.wait_ge(h1_ready, CHUNKS + 1)
                    dve.wait_ge(zt_psum, c + 1)
                    dve.wait_ge(sq_ready, c + 1)
                    nc.vector.scalar_tensor_tensor(out=norm[:, :, :], in0=work[:, :, :], scalar=LEAK, in1=work[:, :, :],
                                                   op0=ALU.mult, op1=ALU.max).then_inc(z_ready, 1)
                if g == 6:
                    dve.wait_ge(zt_split, c + 1)
                    nc.vector.tensor_tensor(cols(z_lo, c), ps_t, cols(z_hi, c).bitcast(F32), ALU.subtract).then_inc(z_done, 1)
                if g == 7:
                    dve.wait_ge(q_split, c + 1)
                    low = cols(z_norm, c)[P // 2:P]
                    nc.vector.scalar_tensor_tensor(out=low, in0=ps_q[P // 2:P], scalar=-0.5, in1=low.bitcast(F32),
                                                   op0=ALU.mult, op1=ALU.subtract).then_inc(q_done, 1)

            def chunk2(c, before):
                for g in range(GROUPS):
                    lower(1, c, g, a_parts2)
                    if before is not None:
                        finish2(before, g)
                    elif g == 1:
                        finish1_a(CHUNKS - 1)
                    elif g == 2:
                        finish1_b(CHUNKS - 1)
                    elif g == 5:
                        finish1_c(CHUNKS - 1)

            dve.wait_ge(small_in[6], DMA)
            chunk2(0, None)
            with dve.Fori(1, CHUNKS) as c:
                chunk2(c, c - 1)
            for g in range(GROUPS):
                finish2(CHUNKS - 1, g)

            dve.sem_inc(row_free, 2)

            def search(i, before):
                dve.drain()
                for k in range(K):
                    wait_apart(dve, row_ready, i * K + (k + 1))
                    nc.vector.max(top8[:, k, :], rows[:, k % 2, :])
                    dve.drain()
                    nc.vector.max_index(idx8[:, k, :], top8[:, k, :], rows[:, k % 2, :]).then_inc(row_free, 1)
                    if k == 2 and before:
                        degrees(i - 1)
                dve.drain()
                nc.vector.tensor_copy(tiles(near, i), idx8[:, :, 0:NEAR])
                nc.vector.tensor_scalar(dist_in[:, :, :], top8[:, :, 0:NEAR], -1.0, SIM_EPS, ALU.mult, ALU.add).then_inc(dist_wanted, 1)

            def degrees(i):
                dve.wait_ge(sim_ready, i + 1)
                nc.vector.tensor_reduce(sim_sum[:, :], tiles(sim, i), AX.X, ALU.add)
                dve.drain()
                nc.vector.tensor_tensor(sim_deg[:, :], sim_sum[:, :], tiles(deg, i), ALU.add).then_inc(deg2_wanted, 1)

            search(0, False)
            with dve.Fori(1, GROUPS) as i:
                search(i, True)
            degrees(GROUPS - 1)

            def lay_indices(c, par):
                nc.vector.tensor_copy(idx_now[:, par, :].rearrange("p (k j) -> p k j", k=K), tiles(near, c)).then_inc(idx_ready, 1)

            def near_sums(c, par):
                dve.wait_ge(rows_scaled, c * K + K)
                dve.wait_ge(near_psum, c + 1)
                rows_at = gathered[:, par].rearrange("p (k j) f -> p k j f", k=K)
                nc.vector.tensor_tensor(rows_at[:, :, 0:2], rows_at[:, :, 0:2], rows_at[:, :, 2:4], ALU.add)
                dve.drain()
                nc.vector.tensor_tensor(near_sum[:, :, :], rows_at[:, :, 0], rows_at[:, :, 1], ALU.add).then_inc(near_ready, 1)

            def product(c):
                dve.wait_ge(y_kept, c + 1)
                dve.wait_ge(w_ready, c + 2 * CHUNKS)
                dve.wait_ge(near_psum, c + 2)
                nc.vector.tensor_tensor(prod_t[:, :], ps_t, cols(y_all, c), ALU.add).then_inc(y3_ready, 1)

            def outputs(c, par, uses):
                dve.wait_ge(w_ready, c + (2 * CHUNKS + 1))
                dve.wait_ge(stored[par], uses * DMA)
                for k in range(K):
                    last = nc.vector.scalar_tensor_tensor(out=out_sb[:, par, k, :], in0=ps_w[:, k, :], scalar=tile_at(d2_col, c * K + k),
                                                          in1=tile_at(x_sb, c * K + k)[:, 0, :], op0=ALU.mult, op1=ALU.add)
                last.then_inc(w_used, 1)

            def chunk3(c, par, out_uses, near_at):
                for g in range(GROUPS):
                    lower(2, c, g, a_parts3)
                    if g == 1 and out_uses is not None:
                        product(c - 3)
                    if g == 5 and out_uses is not None:
                        outputs(c - 3, 1 - par, out_uses)
                    if g == near_at:
                        near_sums(c - EARLY, par)
                        dve.drain()
                        lay_indices(c, par)

            dve.wait_ge(b2_added, GROUPS)
            dve.drain()
            for par in range(2):
                lay_indices(par, par)
            chunk3(EARLY, 0, None, GROUPS - 1)
            chunk3(EARLY + 1, 1, 1, GROUPS - 2)
            with dve.Fori(EARLY // 2 + 1, CHUNKS // 2) as i:
                chunk3(i * 2, 0, i - 1, NEAR_AT)
                chunk3(i * 2 + 1, 1, i, NEAR_AT)
            near_sums(CHUNKS - 2, 0)
            product(CHUNKS - 3)
            outputs(CHUNKS - 3, 1, CHUNKS // 2 - 1)
            product(CHUNKS - 2)
            outputs(CHUNKS - 2, 0, CHUNKS // 2)
            near_sums(CHUNKS - 1, 1)
            product(CHUNKS - 1)
            outputs(CHUNKS - 1, 1, CHUNKS // 2)

        @block.gpsimd
        def _(pool):
            nc.gpsimd.memset(neg_half[:, :], -0.5)
            nc.gpsimd.memset(half[:, :, :], 0.5)
            nc.gpsimd.memset(pick[:, :].bitcast(F32), 0.0)
            nc.gpsimd.memset(zeros[:, :], 0.0)
            pool.drain()
            nc.gpsimd.memset(pick[0:1, :].bitcast(F32), 1.0)
            pool.drain()
            nc.gpsimd.memset(pick[P // 2:P // 2 + 1, :].bitcast(F32), 1.0)
            pool.drain()
            nc.gpsimd.memset(ones[:, :], 1.0).then_inc(consts, 1)

            pool.wait_ge(var_ready, 1)
            nc.gpsimd.tensor_tensor(rstd0[:, :], var_eps[:, :], neg_half[:, :], ALU.pow).then_inc(rstd_ready, 1)

            with pool.Fori(0, CHUNKS) as c:
                pool.wait_ge(pow_wanted, c + 1)
                nc.gpsimd.tensor_tensor(pow_out[:, :, :], pow_in[:, :, :],
                                        neg_half[:, 0:2 * K].rearrange("p (a k) -> p a k", a=2), ALU.pow).then_inc(pow_ready, 1)

            def stage(i, k):
                at = (bass.ds((i * K + k) * P, P) if not isinstance(i, int) else slice((i * K + k) * P, (i * K + k + 1) * P))
                nc.gpsimd.tensor_copy(z_hi_now[:, k, :], z_hi[:, at].bitcast(F32))
                nc.gpsimd.tensor_copy(z_lo_now[:, k, :], z_lo[:, at].bitcast(F32)).then_inc(z_staged, 1)

            def roots(i):
                pool.wait_ge(dist_wanted, i + 1)
                nc.gpsimd.tensor_tensor(dist[:, :, :], dist_in[:, :, :], half[:, :, :], ALU.pow).then_inc(dist_ready, 1)

            def scaled(i, first):
                pool.wait_ge(deg2_wanted, i + 1)
                nc.gpsimd.tensor_tensor(tiles(d2_col, i), sim_deg[:, :], neg_half[:, 0:K], ALU.pow)
                pool.drain()
                if not first:
                    pool.wait_ge(tile_used, i * K)
                    pool.wait_ge(u_stored, i * DMA)
                nc.gpsimd.tensor_tensor(feat_now[:, :, :], tiles(h1, i), over_features(tiles(d2_col, i)),
                                        ALU.mult).then_inc(feat_ready, 1)
                pool.drain()
                pool.dma_start(tiles_of(u_tiles, i), feat_now[:, :, :]).then_inc(u_stored, DMA)
                nc.gpsimd.tensor_copy(tiles(feat_c[0], i), feat_now[:, :, :])
                pool.drain()
                nc.gpsimd.tensor_tensor(tiles(feat_c[1], i), feat_now[:, :, :], tiles(feat_c[0], i).bitcast(F32),
                                        ALU.subtract).then_inc(feat_c_ready, 1)

            def add_b2(i):
                nc.gpsimd.tensor_tensor(tiles(x_sb, i), tiles(x_sb, i), over_tiles(b2_row[:, :]), ALU.add).then_inc(b2_added, 1)

            def step(i, before):
                add_b2(i)
                for k in range(K):
                    pool.wait_ge(pair_ready, (i * K + k + 1) * PAIRS)
                    stage(i + 1, k)
                if before:
                    scaled(i - 1, before == "first")
                roots(i)

            pool.wait_ge(small_in[7], DMA)
            pool.wait_ge(z_done, CHUNKS + 1)
            for k in range(K):
                stage(0, k)
            step(0, None)
            step(1, "first")
            with pool.Fori(2, GROUPS - 1) as i:
                step(i, "later")
            add_b2(GROUPS - 1)
            scaled(GROUPS - 2, False)
            roots(GROUPS - 1)
            scaled(GROUPS - 1, False)

            pool.wait_ge(u_stored, GROUPS * DMA)
            with pool.Fori(0, CHUNKS // 2) as i:
                for par in range(2):
                    wait_apart(pool, idx_ready, i * 2 + (par + 1))
                    for m in range(K * NEAR):
                        nc.gpsimd.indirect_dma_start(
                            out=gathered[:, par, m, :], out_offset=None, in_=u_d,
                            in_offset=bass.IndirectOffsetOnAxis(ap=idx_now[:, par, m:m + 1], axis=0)).then_inc(rows_in[par][m // NEAR], DMA)


def kernel(x, adj, L0_gnn_t, L0_gnn_alpha, L0_gnn_W, L0_gnn_b, L1_gnn_W1, L1_gnn_b1, L1_gnn_W2, L1_gnn_b2):
    import numpy as np
    import concourse.bacc as bacc
    from concourse.bass_utils import run_bass_kernel_spmd

    n, h = x.shape
    blocks = np.asarray(adj).T.reshape(n // CHUNK, K, P, n // CHUNK, CHUNK).transpose(3, 0, 2, 1, 4)
    arrays = {
        "x": np.ascontiguousarray(x),
        "at": np.ascontiguousarray(blocks).reshape(n // CHUNK, n // CHUNK, P, K * CHUNK),
        "alpha": np.ascontiguousarray(np.broadcast_to(np.asarray(L0_gnn_alpha).reshape(1, 1), (P, 1))),
        "wt": np.ascontiguousarray(np.asarray(L0_gnn_W).T),
        "b": np.ascontiguousarray(np.broadcast_to(np.asarray(L0_gnn_b), (P, h))),
        "w1": np.ascontiguousarray(L1_gnn_W1),
        "b1": np.ascontiguousarray(np.broadcast_to(np.asarray(L1_gnn_b1), (P, h))),
        "w2": np.ascontiguousarray(L1_gnn_W2),
        "b2": np.ascontiguousarray(np.broadcast_to(np.asarray(L1_gnn_b2), (P, h))),
        "ident": np.eye(P, dtype=np.float32),
    }
    nc = bacc.Bacc("TRN2", target_bir_lowering=False, num_devices=1)
    ins = [nc.dram_tensor(f"in_{k}", a.shape, mybir.dt.from_np(a.dtype), kind="ExternalInput").ap() for k, a in arrays.items()]
    out = nc.dram_tensor("out", (n, h), F32, kind="ExternalOutput").ap()
    scratch = nc.dram_tensor("scaled_features", (n, h), F32, kind="Internal").ap()
    graph_layers(nc, *ins, out, scratch)
    r = run_bass_kernel_spmd(nc, [{f"in_{k}": a for k, a in arrays.items()}], core_ids=[0])
    return r.results[0]["out"]
```

```python
from contextlib import ExitStack

import concourse.bass as bass
from concourse import mybir

F32 = mybir.dt.float32
F32R = mybir.dt.float32r
U32 = mybir.dt.uint32
ALU = mybir.AluOpType
ACT = mybir.ActivationFunctionType
AX = mybir.AxisListType

P = 128
CHUNK = 512
K = CHUNK // P
SLOTS = 4
NEAR = 4
EARLY = 3
ROW_SLOTS = 3
TOP = 8
LN_EPS = 1e-5
SIM_EPS = 1e-10
LEAK = 0.1
DMA = 16


def graph_layers(nc, x_d, at_d, alpha_d, wt_d, b_d, w1_d, b1_d, w2_d, b2_d, ident_d, out_d, u_d):
    N, H = x_d.shape
    TILES = N // P
    CHUNKS = N // CHUNK
    GROUPS = TILES // K
    LAPS = GROUPS // SLOTS
    SWEEP = CHUNKS * GROUPS
    PAIRS = CHUNKS // 2
    assert H == P and CHUNKS % 2 == 0 and GROUPS == LAPS * SLOTS and PAIRS * 2 == 8

    x_tiles = x_d.rearrange("(t p) f -> p t f", p=P)
    out_tiles = out_d.rearrange("(t p) f -> p t f", p=P)
    u_tiles = u_d.rearrange("(t p) f -> p t f", p=P)

    with ExitStack() as ctx:
        def sb(name, shape, dt=F32):
            return ctx.enter_context(nc.sbuf_tensor(name, shape, dt))

        def sem(name):
            return ctx.enter_context(nc.semaphore(name))

        x_sb = sb("x_sb", [P, TILES, P])
        h1 = sb("h1", [P, TILES, P])
        ring = sb("ring", [P, SLOTS, K, CHUNK])
        ident = sb("ident", [P, P])
        ones = sb("ones", [P, P])
        zeros = sb("zeros", [P, CHUNK], F32R)
        wt = sb("wt", [P, P])
        w1 = sb("w1", [P, P])
        w2 = sb("w2", [P, P])
        b_row = sb("b_row", [P, P])
        b1_row = sb("b1_row", [P, P])
        b2_row = sb("b2_row", [P, P])
        alpha = sb("alpha", [P, 1])
        beta = sb("beta", [P, 1])
        neg_half = sb("neg_half", [P, TILES])
        half = sb("half", [P, K, NEAR])
        stats = sb("stats", [P, TILES, 6])
        mean_var = sb("mean_var", [P, TILES, 2])
        var_eps = sb("var_eps", [P, TILES])
        rstd0 = sb("rstd0", [P, TILES])
        deg = sb("deg", [P, TILES])
        d_col = sb("d_col", [P, TILES])
        d2_col = sb("d2_col", [P, TILES])
        sq_col = sb("sq_col", [P, TILES])
        sim = sb("sim", [P, TILES, NEAR])
        near = sb("near", [P, TILES, NEAR], U32)
        pow_in = sb("pow_in", [P, 2, K])
        pow_out = sb("pow_out", [P, 2, K])
        out_deg = sb("out_deg", [P, K])
        deg_zero = sb("deg_zero", [P, K])
        deg_safe = sb("deg_safe", [P, K])
        inv_deg = sb("inv_deg", [P, K])
        prod_t = sb("prod_t", [P, CHUNK])
        deg_part = sb("deg_part", [P, CHUNK])
        work = sb("work", [P, K, P])
        norm = sb("norm", [P, K, P])
        square = sb("square", [P, K, P])
        z_sq_t = sb("z_sq_t", [P, CHUNK])
        feat_now = sb("feat_now", [P, K, P])
        z_hi_now = sb("z_hi_now", [P, K, P], F32R)
        z_lo_now = sb("z_lo_now", [P, K, P], F32R)
        pick = sb("pick", [P, P], F32R)
        top8 = sb("top8", [P, K, TOP])
        idx8 = sb("idx8", [P, K, TOP], U32)
        dist_in = sb("dist_in", [P, K, NEAR])
        dist = sb("dist", [P, K, NEAR])
        sim_sum = sb("sim_sum", [P, K])
        sim_deg = sb("sim_deg", [P, K])
        idx_now = sb("idx_now", [P, ROW_SLOTS, K * NEAR], U32)

        KB = 1024
        arena = sb("arena", [P, 112 * KB // 4])
        arena_at = nc.sbuf_base - 112 * KB

        def region(name, offset, shape, dt=F32):
            return nc.alloc_sbuf_tensor_at(name, shape, dt, offset=arena_at + offset * KB)

        h_t = region("h_t", 32, [P, N])
        acc = region("acc", 48, [P, K, CHUNK])
        feat_a = region("feat_a", 64, [P, TILES, P])
        feat_b = [region(f"feat_b_{x}", o, [P, TILES, P], F32R) for x, o in (("hi", 0), ("lo", 16))]
        a_parts2 = [region(f"a2_{x}", o, [P, 2, K, CHUNK], F32R) for x, o in (("hi", 80), ("lo", 96))]
        z_hi = region("z_hi", 32, [P, N], F32R)
        z_lo = region("z_lo", 48, [P, N], F32R)
        z_norm = region("z_norm", 64, [P, N], F32R)
        rows = region("rows", 0, [P, 2, N])
        last_tiles = region("last_tiles", 48, [P, K, EARLY, CHUNK])
        feat_c = [region(f"feat_c_{x}", o, [P, TILES, P], F32R) for x, o in (("hi", 80), ("lo", 96))]
        a_parts3 = [region(f"a3_{x}", o, [P, 2, K, CHUNK], F32R) for x, o in (("hi", 0), ("lo", 16))]
        gathered = [region(f"gathered{s}", o, [P, K * NEAR, P]) for s, o in enumerate((32, 40, 72))]
        y_all = region("y_all", 48, [P, N])
        near_sum = region("near_sum", 64, [P, K, P])
        out_sb = region("out_sb", 66, [P, ROW_SLOTS, K, P])

        psum = ctx.enter_context(nc.psum_tensor("psum", [P, 8, CHUNK], F32))
        BANK_W, BANK_DEG = 2, 3
        BANK_T, BANK_Q = 2, 3
        BANK_NEAR = 4
        BANKS3 = (0, 3)
        BANK_PAIRS = 4
        ps_w = psum[:, BANK_W, :].rearrange("p (k f) -> p k f", k=K)
        ps_deg = psum[:, BANK_DEG, :].rearrange("p (k f) -> p k f", k=K)
        ps_t = psum[:, BANK_T, :]
        ps_near = psum[:, BANK_NEAR, :]
        ps_q = psum[:, BANK_Q, :]

        x_in = [sem(f"x_in{g}") for g in range(GROUPS)]
        small_in = {w: sem(f"{w}_in") for w in ("alpha", "ident", "wt", "w1", "w2", "b", "b1", "b2")}
        load_done = [sem(f"load_done{s}") for s in range(SLOTS)]
        pe_groups = sem("pe_groups")
        dve_groups = sem("dve_groups")
        hi_ready = sem("hi_ready")
        tile_in = [sem(f"tile_in{k}") for k in range(K)]
        last_in = [sem(f"last_in{k}") for k in range(K)]
        tile_used = sem("tile_used")
        unread = sem("unread")
        consts = sem("consts")
        var_ready = sem("var_ready")
        rstd_ready = sem("rstd_ready")
        h_norm = sem("h_norm")
        h_ready = sem("h_ready")
        ht_psum = sem("ht_psum")
        ht_ready = sem("ht_ready")
        y1_ready = sem("y1_ready")
        y_ready = sem("y_ready")
        y_kept = sem("y_kept")
        near_psum = sem("near_psum")
        y3_ready = sem("y3_ready")
        w_ready = sem("w_ready")
        w_used = sem("w_used")
        pow_wanted = sem("pow_wanted")
        pow_ready = sem("pow_ready")
        norm_ready = sem("norm_ready")
        h1_ready = sem("h1_ready")
        feat_b_ready = sem("feat_b_ready")
        z_ready = sem("z_ready")
        sq_ready = sem("sq_ready")
        zt_psum = sem("zt_psum")
        zt_split = sem("zt_split")
        z_done = sem("z_done")
        q_psum = sem("q_psum")
        q_split = sem("q_split")
        q_done = sem("q_done")
        z_staged = sem("z_staged")
        pair_ready = sem("pair_ready")
        pair_free = sem("pair_free")
        row_ready = sem("row_ready")
        row_free = sem("row_free")
        dist_wanted = sem("dist_wanted")
        dist_ready = sem("dist_ready")
        sim_ready = sem("sim_ready")
        deg2_wanted = sem("deg2_wanted")
        feat_ready = sem("feat_ready")
        feat_c_hi = sem("feat_c_hi")
        feat_c_ready = sem("feat_c_ready")
        u_stored = sem("u_stored")
        rows_in = [[sem(f"rows_in{s}_{k}") for k in range(K)] for s in range(ROW_SLOTS)]
        idx_ready = sem("idx_ready")
        rows_scaled = sem("rows_scaled")
        near_ready = sem("near_ready")
        b2_added = sem("b2_added")
        stored = [sem(f"stored{s}") for s in range(ROW_SLOTS)]

        def free_at_first(eng, *whats):
            for what in whats:
                eng.sem_inc(what, 1)

        at_tiles = at_d.rearrange("c g p (k n) -> g k p c n", k=K)

        def tiles(t, c):
            return t[:, bass.ds(c * K, K)] if not isinstance(c, int) else t[:, c * K:(c + 1) * K]

        def tile_at(t, i):
            return t[:, bass.ds(i, 1)] if not isinstance(i, int) else t[:, i:i + 1]

        def cols(t, c):
            return t[:, bass.ds(c * CHUNK, CHUNK)] if not isinstance(c, int) else t[:, c * CHUNK:(c + 1) * CHUNK]

        def over_features(v):
            return v.unsqueeze(2).to_broadcast([P, K, P])

        def over_tiles(v):
            return v.unsqueeze(1).to_broadcast([P, K, P])

        def wait_apart(eng, what, value):
            eng.wait_ge(what, value)
            eng.sem_inc(unread, 1)

        def tiles_of(d, c):
            return tiles(d, c)

        def early_tile(k):
            return ring[:, SLOTS // 2 + k % 2, 0:EARLY, :]

        def arrived(eng, sweep, c, g):
            before = sweep * CHUNKS * LAPS - (EARLY * LAPS if sweep == 2 else 0)
            eng.wait_ge(load_done[g % SLOTS], (c * LAPS + (g // SLOTS + 1 + before)) * DMA)

        def split_count(sweep, c, g):
            return c * GROUPS + (g + 1 + ((sweep - 1) * SWEEP - (EARLY * GROUPS if sweep == 2 else 0)))

        block = ctx.enter_context(nc.Block())

        @block.sync
        def _(sp):
            def load(sweep, c, g):
                n = c * GROUPS + g + (sweep * SWEEP - (EARLY * GROUPS if sweep == 2 else 0))
                fresh = isinstance(n, int) and n < SLOTS
                if not fresh and (sweep == 0 or (isinstance(n, int) and n - SLOTS < SWEEP)):
                    sp.wait_ge(pe_groups, n - SLOTS + 1)
                if not fresh:
                    sp.wait_ge(dve_groups, n - SLOTS + 1)
                sp.dma_start(ring[:, g % SLOTS].rearrange("p k n -> p (k n)"),
                             at_d[c, g]).then_inc(load_done[g % SLOTS], DMA)

            for g in range(GROUPS):
                sp.dma_start(x_sb[:, g * K:(g + 1) * K, :], x_tiles[:, g * K:(g + 1) * K, :]).then_inc(x_in[g], DMA)
                if g % 2 == 1:
                    load(0, 0, g // 2)

            for sweep in range(2):
                for g in range(GROUPS // 2 if sweep == 0 else 0, GROUPS):
                    load(sweep, 0, g)
                with sp.Fori(1, CHUNKS) as c:
                    for g in range(GROUPS):
                        load(sweep, c, g)

            def load_tiles(i, first):
                for k in range(K):
                    if not first or k >= 2:
                        sp.wait_ge(tile_used, i * K + k - 1)
                    sp.dma_start(early_tile(k), at_tiles[i, k][:, 0:EARLY, :]).then_inc(tile_in[k], DMA)

            sp.wait_ge(dve_groups, 2 * SWEEP)
            for g in range(SLOTS // 2):
                load(2, EARLY, g)
            load_tiles(0, True)
            with sp.Fori(1, GROUPS - 1) as i:
                load_tiles(i, False)
            sp.wait_ge(pair_ready, TILES * PAIRS)
            for k in range(K):
                if k == K - 1:
                    sp.wait_ge(u_stored, GROUPS * DMA)
                sp.dma_start(last_tiles[:, k], at_tiles[GROUPS - 1, k][:, 0:EARLY, :]).then_inc(last_in[k], DMA)
            sp.wait_ge(tile_used, TILES - K)
            for g in range(SLOTS // 2, GROUPS):
                load(2, EARLY, g)
            with sp.Fori(EARLY + 1, CHUNKS) as c:
                for g in range(GROUPS):
                    load(2, c, g)

        @block.tensor
        def _(pe):
            def transposes(g):
                pe.wait_ge(h_ready, g + 1)
                if g >= 2:
                    pe.wait_ge(ht_ready, g - 1)
                for k in range(K):
                    last = nc.tensor.transpose(psum[:, BANK_NEAR + g % 2, k * P:(k + 1) * P], feat_a[:, g * K + k, :], ident[:, :])
                last.then_inc(ht_psum, 1)

            def stream(c, bank, between):
                for g in range(GROUPS):
                    if isinstance(c, int) and c == 0:
                        transposes(g)
                    arrived(pe, 0, c, g)
                    for k in range(K):
                        t = g * K + k
                        last = nc.tensor.matmul(psum[:, bank, :], feat_a[:, t, :], ring[:, g % SLOTS, k, :],
                                                start=(t == 0), stop=(t == TILES - 1))
                    last.then_inc(pe_groups, 1)
                    if between is not None:
                        between(g)

            def stream_parts(sweep, c, bank, feat, a_parts, between):
                for g in range(GROUPS):
                    if sweep == 1 and isinstance(c, int) and c == 0:
                        pe.wait_ge(feat_b_ready, g + 2)
                    if sweep == 2 and g == 0 and not (isinstance(c, int) and c == EARLY):
                        pe.wait_ge(y_kept, c - 1)
                    if sweep == 2 and isinstance(c, int) and c == EARLY:
                        pe.wait_ge(feat_c_ready, g + 1)
                    pe.wait_ge(hi_ready, split_count(sweep, c, g))
                    for k in range(K):
                        for m in range(2):
                            nc.tensor.matmul(psum[:, bank, :], feat[m][:, g * K + k, :], a_parts[0][:, g % 2, k, :],
                                             start=(g == k == m == 0), stop=False)
                    pe.wait_ge(dve_groups, split_count(sweep, c, g) + SWEEP)
                    for k in range(K):
                        last = nc.tensor.matmul(psum[:, bank, :], feat[0][:, g * K + k, :], a_parts[1][:, g % 2, k, :],
                                                start=False, stop=(g == GROUPS - 1 and k == K - 1))
                    last.then_inc(pe_groups, 1)
                    if between is not None:
                        between(g)

            def weights(n, rhs):
                pe.wait_ge(w_used, n + 1)
                for k in range(K):
                    last = nc.tensor.matmul(ps_w[:, k, :], prod_t[:, k * P:(k + 1) * P], rhs[:, :], start=True, stop=True)
                return last

            def finish1(c):
                pe.wait_ge(y1_ready, c + 1)
                weights(c, wt)
                for k in range(K):
                    last = nc.tensor.transpose(ps_deg[:, k, :], deg_part[:, k * P:(k + 1) * P], ident[:, :])
                last.then_inc(w_ready, 1)

            def finish2(c, g):
                if g == 0:
                    pe.wait_ge(y_ready, c + 1)
                    pe.wait_ge(z_done, c + 1)
                    weights(c + CHUNKS, w1).then_inc(w_ready, 1)
                if g == 3:
                    pe.wait_ge(z_ready, c + 1)
                    for k in range(K):
                        last = nc.tensor.transpose(ps_t[:, k * P:(k + 1) * P], norm[:, k, :], ident[:, :])
                    last.then_inc(zt_psum, 1)
                if g == 5:
                    pe.wait_ge(zt_split, c + 1)
                    pe.wait_ge(q_done, c + 1)
                    nc.tensor.matmul(ps_q, ones[:, :], z_sq_t[:, :], start=True, stop=True).then_inc(q_psum, 1)

            def turn_near(c):
                pe.wait_ge(near_ready, c + (ROW_SLOTS + 1))
                pe.wait_ge(y3_ready, c + 1)
                for k in range(K):
                    last = nc.tensor.transpose(ps_near[:, k * P:(k + 1) * P], near_sum[:, k, :], ident[:, :])
                last.then_inc(near_psum, 1)

            def weigh3(c):
                pe.wait_ge(y3_ready, c + 2)
                weights(c + 2 * CHUNKS, w2).then_inc(w_ready, 1)

            def even3(i, g):
                if g == 1:
                    weigh3(i * 3 - 6)
                if g == 4:
                    turn_near(i * 3 - 5)
                if g == 6:
                    weigh3(i * 3 - 5)

            def odd3(i, g):
                if g == 0:
                    turn_near(i * 3 - 4)
                if g == 2:
                    weigh3(i * 3 - 4)
                if g == 6:
                    turn_near(i * 3 - 3)

            free_at_first(pe, zt_psum, q_psum, near_psum)

            def run_sweep(stream, before, finish):
                stream(0, 0, before)
                with pe.Fori(0, CHUNKS // 2 - 1) as i:
                    for j in range(1, 3):
                        stream(i * 2 + j, j % 2, lambda g, c=i * 2 + j: finish(c, g))
                stream(CHUNKS - 1, 1, lambda g: finish(CHUNKS - 1, g))

            def first1(g):
                if g == GROUPS - 1:
                    for name in ("wt", "w1", "w2"):
                        pe.wait_ge(small_in[name], DMA)
                    pe.wait_ge(consts, 1)

            pe.wait_ge(small_in["ident"], DMA)
            run_sweep(stream, first1, lambda c, g: finish1(c - 1) if g == 0 else None)
            finish1(CHUNKS - 1)
            run_sweep(lambda c, bank, between: stream_parts(1, c, bank, feat_b, a_parts2, between),
                      None, lambda c, g: finish2(c - 1, g))

            def pair(i, k, q):
                pe.wait_ge(pair_free, (i * K + k) * PAIRS + (q + 1))
                parts = ((pick[:, :], z_norm), (z_hi_now[:, k, :], z_hi), (z_hi_now[:, k, :], z_lo), (z_lo_now[:, k, :], z_hi))
                for m, (lhs, rhs) in enumerate(parts):
                    for b in range(2):
                        last = nc.tensor.matmul(psum[:, BANK_PAIRS + 2 * (q % 2) + b, :], lhs, cols(rhs, 2 * q + b),
                                                start=(m == 0), stop=(m == len(parts) - 1))
                last.then_inc(pair_ready, 1)

            finish2(CHUNKS - 1, 0)
            pe.wait_ge(z_staged, 1)
            pe.wait_ge(q_done, CHUNKS - 1)
            for q in range(2):
                pair(0, 0, q)
            finish2(CHUNKS - 1, 3)
            pair(0, 0, 2)
            finish2(CHUNKS - 1, 5)
            pe.wait_ge(w_used, 2 * CHUNKS + 1)
            pe.wait_ge(z_done, CHUNKS + 1)
            for b in range(EARLY):
                nc.tensor.matmul(psum[:, b, :], zeros[:, 0:P], zeros[:, :], start=True, stop=False, skip_group_check=True)
            pe.wait_ge(q_done, CHUNKS + 1)

            def early(i, k, tile):
                pe.wait_ge(feat_ready, i + 1)
                for b in range(EARLY):
                    last = nc.tensor.matmul(psum[:, b, :], feat_now[:, k, :], tile[:, b, :],
                                            start=False, stop=False, skip_group_check=True)
                last.then_inc(tile_used, 1)

            def distances(i, lag):
                for k in range(K):
                    pe.wait_ge(z_staged, i * K + (k + 1))
                    for q in range(PAIRS):
                        if isinstance(i, int) and i == k == 0 and q < 3:
                            continue
                        pair(i, k, q)
                    if lag:
                        pe.wait_ge(tile_in[k], (i - 1) * DMA)
                        early(i - 2, k, early_tile(k))

            for i in range(2):
                distances(i, False)
            with pe.Fori(2, GROUPS) as i:
                distances(i, True)
            for k in range(K):
                pe.wait_ge(tile_in[k], (GROUPS - 1) * DMA)
                early(GROUPS - 2, k, early_tile(k))

            def last_early(g):
                if g < K:
                    pe.wait_ge(last_in[g], DMA)
                    early(GROUPS - 1, g, last_tiles[:, g])

            stream_parts(2, EARLY, BANKS3[1], feat_c, a_parts3, last_early)
            pe.wait_ge(pair_free, TILES * PAIRS + 2)
            turn_near(0)
            with pe.Fori(2, CHUNKS // 2) as i:
                stream_parts(2, i * 2, BANKS3[0], feat_c, a_parts3, lambda g: even3(i, g))
                stream_parts(2, i * 2 + 1, BANKS3[1], feat_c, a_parts3, lambda g: odd3(i, g))
            weigh3(CHUNKS - 2)
            turn_near(CHUNKS - 1)
            weigh3(CHUNKS - 1)

        @block.scalar
        def _(act):
            act.dma_start(alpha[:, :], alpha_d).then_inc(small_in["alpha"], DMA)
            act.dma_start(ident[:, :], ident_d).then_inc(small_in["ident"], DMA)
            free_at_first(act, h1_ready, sq_ready)
            for slot in range(ROW_SLOTS):
                act.sem_inc(stored[slot], DMA)

            def h_of(g):
                act.wait_ge(h_norm, g + 1)
                nc.scalar.activation(feat_a[:, g * K:(g + 1) * K, :], h1[:, g * K:(g + 1) * K, :], ACT.Relu).then_inc(h_ready, 1)

            def ht_of(g):
                act.wait_ge(ht_psum, g + 1)
                nc.scalar.activation(cols(h_t, g), psum[:, BANK_NEAR + g % 2, :], ACT.Copy, scale=beta[:, 0:1]).then_inc(ht_ready, 1)

            for g in range(GROUPS):
                h_of(g)
                if g >= 1:
                    ht_of(g - 1)
                if g == 2:
                    for name, to, of in (("wt", wt, wt_d), ("w1", w1, w1_d), ("w2", w2, w2_d),
                                         ("b", b_row, b_d), ("b1", b1_row, b1_d), ("b2", b2_row, b2_d)):
                        act.dma_start(to[:, :], of).then_inc(small_in[name], DMA)
            ht_of(GROUPS - 1)

            def features(c):
                act.wait_ge(norm_ready, c + 1)
                nc.scalar.activation(tiles(h1, c), norm[:, :, :], ACT.Relu)
                nc.scalar.activation(tiles(d_col, c), pow_out[:, 1, :], ACT.Copy)
                act.wait_ge(feat_b_ready, c + 1)
                for k in range(K):
                    nc.scalar.activation(feat_now[:, k, :], norm[:, k, :], ACT.Relu, scale=pow_out[:, 1, k:k + 1])
                act.drain()
                nc.scalar.activation(tiles(feat_b[0], c), feat_now[:, :, :], ACT.Copy).then_inc(h1_ready, 1)

            with act.Fori(0, CHUNKS - 1) as c:
                features(c)

            def upper(sweep, c, g, a_parts):
                act.wait_ge(pe_groups, split_count(sweep, c, g) + (SWEEP - 2))
                arrived(act, sweep, c, g)
                nc.scalar.activation(a_parts[0][:, g % 2], ring[:, g % SLOTS], ACT.Copy).then_inc(hi_ready, 1)

            def finish2(c, par, g):
                if g == 1:
                    act.wait_ge(pe_groups, c * GROUPS + (SWEEP + GROUPS))
                    act.wait_ge(w_ready, c + CHUNKS)
                    nc.scalar.activation(prod_t[:, :], psum[:, par, :], ACT.Copy).then_inc(y_ready, 1)
                if g == 4:
                    act.drain()
                    wait_apart(act, z_ready, c + 1)
                    for k in range(K):
                        last = nc.scalar.activation(square[:, k, :], norm[:, k, :], ACT.Square,
                                                    accum_out=tile_at(sq_col, c * K + k))
                    last.then_inc(sq_ready, 1)
                if g == 5:
                    act.wait_ge(zt_psum, c + 2)
                    act.wait_ge(q_psum, c + 1)
                    nc.scalar.activation(cols(z_hi, c), ps_t, ACT.Copy)
                    nc.scalar.activation(z_sq_t[:, :], ps_t, ACT.Square).then_inc(zt_split, 1)
                if g == 7:
                    act.wait_ge(q_psum, c + 2)
                    nc.scalar.activation(cols(z_norm, c), ps_q, ACT.Copy, scale=-0.5).then_inc(q_split, 1)

            def chunk2(c, before, par):
                for g in range(GROUPS):
                    upper(1, c, g, a_parts2)
                    if before is not None:
                        finish2(before, par, g)
                    elif g == 4:
                        features(CHUNKS - 1)

            chunk2(0, None, None)
            with act.Fori(0, CHUNKS // 2 - 1) as i:
                chunk2(i * 2 + 1, i * 2, 0)
                chunk2(i * 2 + 2, i * 2 + 1, 1)
            chunk2(CHUNKS - 1, CHUNKS - 2, 0)

            def row_pair(i, k, q):
                if isinstance(i, int):
                    act.wait_ge(pair_ready, (i * K + k) * PAIRS + (q + 1))
                else:
                    wait_apart(act, pair_ready, (i * K + k) * PAIRS + (q + 1))
                nc.scalar.activation(rows[:, k % 2, q * 2 * CHUNK:(q + 1) * 2 * CHUNK],
                                     psum[:, BANK_PAIRS + 2 * (q % 2):BANK_PAIRS + 2 * (q % 2) + 2, :].rearrange("p b n -> p (b n)"),
                                     ACT.Relu, scale=-2.0, bias=tile_at(sq_col, i * K + k)).then_inc(pair_free, 1)

            act.sem_inc(pair_free, 2)
            finish2(CHUNKS - 1, 1, 1)
            act.drain()
            act.wait_ge(row_free, 1)
            row_pair(0, 0, 0)
            finish2(CHUNKS - 1, 1, 4)
            finish2(CHUNKS - 1, 1, 5)
            row_pair(0, 0, 1)
            row_pair(0, 0, 2)
            finish2(CHUNKS - 1, 1, 7)
            act.wait_ge(q_done, CHUNKS + 1)
            act.drain()

            def similarities(i):
                act.wait_ge(dist_ready, i + 1)
                nc.scalar.activation(tiles(sim, i), dist[:, :, :], ACT.Exp, scale=-0.5).then_inc(sim_ready, 1)

            def rows_of(i, before):
                for k in range(K):
                    act.wait_ge(row_free, i * K + (k + 1))
                    for half_row in range(2):
                        for q in range(half_row * PAIRS // 2, (half_row + 1) * PAIRS // 2):
                            if not (isinstance(i, int) and i == k == 0 and q < 3):
                                row_pair(i, k, q)
                        act.drain()
                        part = rows[:, k % 2, half_row * N // 2:(half_row + 1) * N // 2]
                        last = nc.scalar.activation(part, part, ACT.Copy, scale=-1.0)
                    last.then_inc(row_ready, 1)
                    if k == 1 and before:
                        similarities(i - 1)

            rows_of(0, False)
            with act.Fori(1, GROUPS) as i:
                rows_of(i, True)
            similarities(GROUPS - 1)

            def keep(c, bank):
                nc.scalar.activation(cols(y_all, c), psum[:, bank, :], ACT.Copy).then_inc(y_kept, 1)

            def store_out(c, slot):
                act.wait_ge(w_used, c + (2 * CHUNKS + 2))
                act.dma_start(tiles_of(out_tiles, c), out_sb[:, slot]).then_inc(stored[slot], DMA)

            def scale_rows(c, slot, uses, k):
                if isinstance(uses, int):
                    act.wait_ge(rows_in[slot][k], (uses + 1) * NEAR * DMA)
                else:
                    wait_apart(act, rows_in[slot][k], (uses + 1) * (NEAR * DMA))
                for j in range(NEAR):
                    row = gathered[slot][:, k * NEAR + j, :]
                    last = nc.scalar.activation(row, row, ACT.Copy, scale=tile_at(sim, c * K + k)[:, 0, j:j + 1])
                last.then_inc(rows_scaled, 1)

            def scale_rows_with(g, at, c, slot, uses):
                for k in range(K):
                    if g == min(at - 2 + k, at):
                        scale_rows(c, slot, uses, k)

            act.wait_ge(row_free, TILES + 2)
            for g in range(GROUPS):
                upper(2, EARLY, g, a_parts3)
                if g == K:
                    act.wait_ge(tile_used, TILES)
                    for b in range(EARLY):
                        keep(b, b)
                scale_rows_with(g, GROUPS - 1, 0, 0, 0)

            def keep_with(g, c, bank):
                if g == 1:
                    act.wait_ge(pe_groups, split_count(2, c, GROUPS - 1) + SWEEP)
                    keep(c, bank)

            with act.Fori(2, CHUNKS // 2) as i:
                for g in range(GROUPS):
                    upper(2, i * 2, g, a_parts3)
                    keep_with(g, i * 2 - 1, BANKS3[1])
                    scale_rows_with(g, 2, i * 3 - 5, 1, i - 2)
                    scale_rows_with(g, 6, i * 3 - 4, 2, i - 2)
                    if g == 4:
                        store_out(i * 3 - 6, 0)
                for g in range(GROUPS):
                    upper(2, i * 2 + 1, g, a_parts3)
                    keep_with(g, i * 2, BANKS3[0])
                    scale_rows_with(g, 4, i * 3 - 3, 0, i - 1)
                    if g == 1:
                        store_out(i * 3 - 5, 1)
                    if g == 5:
                        store_out(i * 3 - 4, 2)
            for k in range(K):
                scale_rows(CHUNKS - 1, 1, (CHUNKS - 1) // ROW_SLOTS, k)
            act.wait_ge(pe_groups, split_count(2, CHUNKS - 1, GROUPS - 1) + SWEEP)
            keep(CHUNKS - 1, BANKS3[1])
            store_out(CHUNKS - 2, 0)
            store_out(CHUNKS - 1, 1)
            for slot in range(ROW_SLOTS):
                act.wait_ge(stored[slot], (len(range(slot, CHUNKS, ROW_SLOTS)) + 1) * DMA)

        @block.vector
        def _(dve):
            free_at_first(dve, w_used, z_done, q_done, y3_ready, feat_b_ready)

            def variances(g):
                dve.wait_ge(x_in[g], DMA)
                for t in range(g * K, (g + 1) * K):
                    nc.vector.bn_stats(stats[:, t, :], x_sb[:, t, :])
                dve.drain()
                for t in range(g * K, (g + 1) * K):
                    nc.vector.bn_aggr(mean_var[:, t, :], stats[:, t, :])
                dve.drain()
                nc.vector.tensor_scalar(tiles(var_eps, g), tiles(mean_var, g)[:, :, 1], LN_EPS, None, ALU.add).then_inc(var_ready, 1)

            def normalise(g):
                dve.wait_ge(rstd_ready, g + 1)
                for t in range(g * K, (g + 1) * K):
                    last = nc.vector.tensor_scalar(h1[:, t, :], x_sb[:, t, :], mean_var[:, t, 0:1], rstd0[:, t:t + 1],
                                                   ALU.subtract, ALU.mult)
                last.then_inc(h_norm, 1)

            variances(0)
            dve.wait_ge(small_in["alpha"], DMA)
            nc.vector.tensor_scalar(beta[:, :], alpha[:, :], -1.0, 1.0, ALU.mult, ALU.add)
            for g in range(1, SLOTS):
                variances(g)
                normalise(g - 1)

            def row_sums(c, g):
                dve.drain()
                arrived(dve, 0, c, g)
                a = acc[:, :, :].rearrange("p k n -> p (k n)")
                r = ring[:, g % SLOTS].rearrange("p k n -> p (k n)")
                if g == 0:
                    nc.vector.tensor_copy(a, r).then_inc(dve_groups, 1)
                else:
                    nc.vector.tensor_tensor(a, a, r, ALU.add).then_inc(dve_groups, 1)

            def fold_sums():
                dve.drain()
                nc.vector.tensor_tensor(acc[:, 0:2, :], acc[:, 0:2, :], acc[:, 2:4, :], ALU.add)
                dve.drain()
                nc.vector.tensor_tensor(deg_part[:, :], acc[:, 0, :], acc[:, 1, :], ALU.add)

            def mix(c, par):
                dve.wait_ge(pe_groups, (c + 1) * GROUPS)
                nc.vector.scalar_tensor_tensor(out=prod_t[:, :], in0=psum[:, par, :], scalar=alpha[:, 0:1], in1=cols(h_t, c),
                                               op0=ALU.mult, op1=ALU.add).then_inc(y1_ready, 1)

            def finish1_a(c):
                dve.wait_ge(w_ready, c + 1)
                nc.vector.tensor_reduce(pow_in[:, 1, :], ps_deg, AX.X, ALU.add)
                dve.drain()
                nc.vector.tensor_copy(tiles(deg, c), pow_in[:, 1, :])
                nc.vector.tensor_scalar(out_deg[:, :], pow_in[:, 1, :], alpha[:, 0:1], beta[:, 0:1], ALU.mult, ALU.add)
                dve.drain()
                nc.vector.tensor_scalar(deg_zero[:, :], out_deg[:, :], 0.0, None, ALU.is_equal)
                dve.drain()
                nc.vector.tensor_tensor(deg_safe[:, :], out_deg[:, :], deg_zero[:, :], ALU.add)
                dve.drain()
                nc.vector.reciprocal(inv_deg[:, :], deg_safe[:, :])
                nc.vector.tensor_scalar(deg_zero[:, :], deg_zero[:, :], -1.0, 1.0, ALU.mult, ALU.add)
                dve.drain()
                nc.vector.tensor_tensor(inv_deg[:, :], inv_deg[:, :], deg_zero[:, :], ALU.mult)
                dve.drain()
                nc.vector.tensor_tensor(work[:, :, :], ps_w, over_features(inv_deg[:, :]), ALU.mult).then_inc(w_used, 1)

            def finish1_b(c):
                dve.drain()
                nc.vector.tensor_tensor(work[:, :, :], work[:, :, :], over_tiles(b_row[:, :]), ALU.add)
                dve.drain()
                nc.vector.scalar_tensor_tensor(out=tiles(x_sb, c), in0=work[:, :, :], scalar=0.0, in1=tiles(x_sb, c),
                                               op0=ALU.max, op1=ALU.add)
                dve.drain()
                for k in range(K):
                    nc.vector.bn_stats(stats[:, k, :], tile_at(x_sb, c * K + k)[:, 0])
                dve.drain()
                for k in range(K):
                    nc.vector.bn_aggr(mean_var[:, k, :], stats[:, k, :])
                dve.drain()
                dve.wait_ge(h1_ready, c + 1)
                nc.vector.tensor_scalar(pow_in[:, 0, :], mean_var[:, 0:K, 1], LN_EPS, None, ALU.add).then_inc(pow_wanted, 1)

            def finish1_c(c):
                dve.wait_ge(pow_ready, c + 1)
                for k in range(K):
                    last = nc.vector.tensor_scalar(norm[:, k, :], tile_at(x_sb, c * K + k)[:, 0], mean_var[:, k, 0:1],
                                                   pow_out[:, 0, k:k + 1], ALU.subtract, ALU.mult)
                last.then_inc(norm_ready, 1)

            def finish1_d(c):
                dve.wait_ge(h1_ready, c + 2)
                nc.vector.tensor_tensor(tiles(feat_b[1], c), feat_now[:, :, :], tiles(feat_b[0], c).bitcast(F32),
                                        ALU.subtract).then_inc(feat_b_ready, 1)


            def sums_of(c, before, par=None):
                if before is not None:
                    mix(before, par)
                for g in range(GROUPS):
                    row_sums(c, g)
                    if before is None and g < GROUPS - SLOTS:
                        variances(g + SLOTS)
                    if before is None and g <= GROUPS - SLOTS:
                        normalise(g + SLOTS - 1)
                    if before is not None and g == 1:
                        finish1_a(before)
                        finish1_b(before)
                    if before is not None and g == 2:
                        finish1_c(before)
                    if before is not None and g == 4:
                        finish1_d(before)
                if not isinstance(c, int) or c < CHUNKS - 1:
                    fold_sums()

            sums_of(0, None)
            dve.wait_ge(small_in["b"], DMA)
            dve.wait_ge(ht_ready, GROUPS)
            with dve.Fori(0, CHUNKS // 2 - 1) as i:
                sums_of(i * 2 + 1, i * 2, 0)
                sums_of(i * 2 + 2, i * 2 + 1, 1)
            sums_of(CHUNKS - 1, CHUNKS - 2, 0)

            def lower(sweep, c, g, a_parts):
                dve.wait_ge(hi_ready, split_count(sweep, c, g))
                nc.vector.tensor_tensor(a_parts[1][:, g % 2], ring[:, g % SLOTS], a_parts[0][:, g % 2].bitcast(F32),
                                        ALU.subtract).then_inc(dve_groups, 1)

            def finish2(c, g):
                if g == 2:
                    dve.drain()
                    dve.wait_ge(w_ready, c + (CHUNKS + 1))
                    for k in range(K):
                        last = nc.vector.scalar_tensor_tensor(out=work[:, k, :], in0=ps_w[:, k, :], scalar=tile_at(d_col, c * K + k),
                                                              in1=b1_row[:, :], op0=ALU.mult, op1=ALU.add)
                    last.then_inc(w_used, 1)
                    dve.drain()
                    dve.wait_ge(h1_ready, CHUNKS + 1)
                    dve.wait_ge(zt_psum, c + 1)
                    dve.wait_ge(sq_ready, c + 1)
                    nc.vector.scalar_tensor_tensor(out=norm[:, :, :], in0=work[:, :, :], scalar=LEAK, in1=work[:, :, :],
                                                   op0=ALU.mult, op1=ALU.max).then_inc(z_ready, 1)
                if g == 6:
                    dve.wait_ge(zt_split, c + 1)
                    nc.vector.tensor_tensor(cols(z_lo, c), ps_t, cols(z_hi, c).bitcast(F32), ALU.subtract).then_inc(z_done, 1)
                if g == 7:
                    dve.wait_ge(q_split, c + 1)
                    low = cols(z_norm, c)[P // 2:P]
                    nc.vector.scalar_tensor_tensor(out=low, in0=ps_q[P // 2:P], scalar=-0.5, in1=low.bitcast(F32),
                                                   op0=ALU.mult, op1=ALU.subtract).then_inc(q_done, 1)

            def chunk2(c, before):
                for g in range(GROUPS):
                    if before is None and g == 0:
                        fold_sums()
                        mix(CHUNKS - 1, 1)
                    lower(1, c, g, a_parts2)
                    if before is not None:
                        finish2(before, g)
                    elif g == 1:
                        finish1_a(CHUNKS - 1)
                    elif g == 2:
                        finish1_b(CHUNKS - 1)
                    elif g == 3:
                        finish1_c(CHUNKS - 1)
                    elif g == 5:
                        finish1_d(CHUNKS - 1)

            dve.wait_ge(small_in["b1"], DMA)
            chunk2(0, None)
            with dve.Fori(1, CHUNKS) as c:
                chunk2(c, c - 1)
            dve.sem_inc(row_free, 2)
            for g in range(GROUPS):
                finish2(CHUNKS - 1, g)


            def search(i, before):
                dve.drain()
                for k in range(K):
                    wait_apart(dve, row_ready, i * K + (k + 1))
                    nc.vector.max(top8[:, k, :], rows[:, k % 2, :])
                    dve.drain()
                    nc.vector.max_index(idx8[:, k, :], top8[:, k, :], rows[:, k % 2, :]).then_inc(row_free, 1)
                    if k == 2 and before:
                        degrees(i - 1)
                dve.drain()
                nc.vector.tensor_copy(tiles(near, i), idx8[:, :, 0:NEAR])
                nc.vector.tensor_scalar(dist_in[:, :, :], top8[:, :, 0:NEAR], -1.0, SIM_EPS, ALU.mult, ALU.add).then_inc(dist_wanted, 1)

            def degrees(i):
                dve.wait_ge(sim_ready, i + 1)
                nc.vector.tensor_reduce(sim_sum[:, :], tiles(sim, i), AX.X, ALU.add)
                dve.drain()
                nc.vector.tensor_tensor(sim_deg[:, :], sim_sum[:, :], tiles(deg, i), ALU.add).then_inc(deg2_wanted, 1)

            search(0, False)
            with dve.Fori(1, GROUPS) as i:
                search(i, True)
            degrees(GROUPS - 1)

            def near_sums(c, slot):
                dve.wait_ge(rows_scaled, c * K + K)
                dve.wait_ge(near_psum, c + 1)
                rows_at = gathered[slot][:, :, :].rearrange("p (k j) f -> p k j f", k=K)
                nc.vector.tensor_tensor(rows_at[:, :, 0:2], rows_at[:, :, 0:2], rows_at[:, :, 2:4], ALU.add)
                dve.drain()
                nc.vector.tensor_tensor(near_sum[:, :, :], rows_at[:, :, 0], rows_at[:, :, 1], ALU.add).then_inc(near_ready, 1)

            def product(c):
                dve.wait_ge(y_kept, c + 1)
                dve.wait_ge(w_ready, c + 2 * CHUNKS)
                dve.wait_ge(near_psum, c + 2)
                nc.vector.tensor_tensor(prod_t[:, :], ps_near, cols(y_all, c), ALU.add).then_inc(y3_ready, 1)

            def outputs(c, slot, uses):
                dve.wait_ge(w_ready, c + (2 * CHUNKS + 1))
                dve.wait_ge(stored[slot], (uses + 1) * DMA)
                for k in range(K):
                    last = nc.vector.scalar_tensor_tensor(out=out_sb[:, slot, k, :], in0=ps_w[:, k, :], scalar=tile_at(d2_col, c * K + k),
                                                          in1=tile_at(x_sb, c * K + k)[:, 0, :], op0=ALU.mult, op1=ALU.add)
                last.then_inc(w_used, 1)

            def even3(i, g):
                if g == 0:
                    product(i * 3 - 6)
                if g == 2:
                    outputs(i * 3 - 6, 0, i - 2)
                if g == 3:
                    near_sums(i * 3 - 5, 1)
                if g == 5:
                    product(i * 3 - 5)
                if g == 7:
                    outputs(i * 3 - 5, 1, i - 2)
                    near_sums(i * 3 - 4, 2)

            def odd3(i, g):
                if g == 1:
                    product(i * 3 - 4)
                if g == 3:
                    outputs(i * 3 - 4, 2, i - 2)
                if g == 5:
                    near_sums(i * 3 - 3, 0)

            dve.wait_ge(b2_added, GROUPS)
            dve.sem_inc(near_ready, ROW_SLOTS)
            for g in range(GROUPS):
                lower(2, EARLY, g, a_parts3)
            near_sums(0, 0)
            with dve.Fori(2, CHUNKS // 2) as i:
                for g in range(GROUPS):
                    lower(2, i * 2, g, a_parts3)
                    even3(i, g)
                for g in range(GROUPS):
                    lower(2, i * 2 + 1, g, a_parts3)
                    odd3(i, g)
            product(CHUNKS - 2)
            near_sums(CHUNKS - 1, 1)
            outputs(CHUNKS - 2, 0, (CHUNKS - 2) // ROW_SLOTS)
            product(CHUNKS - 1)
            outputs(CHUNKS - 1, 1, (CHUNKS - 1) // ROW_SLOTS)

        @block.gpsimd
        def _(pool):
            nc.gpsimd.memset(neg_half[:, :], -0.5)
            pool.drain()
            for g in range(GROUPS):
                pool.wait_ge(var_ready, g + 1)
                nc.gpsimd.tensor_tensor(tiles(rstd0, g), tiles(var_eps, g), tiles(neg_half, g), ALU.pow).then_inc(rstd_ready, 1)
            nc.gpsimd.memset(half[:, :, :], 0.5)
            nc.gpsimd.memset(pick[:, :].bitcast(F32), 0.0)
            nc.gpsimd.memset(zeros[:, :].bitcast(F32), 0.0)
            pool.drain()
            nc.gpsimd.memset(pick[0:1, :].bitcast(F32), 1.0)
            pool.drain()
            nc.gpsimd.memset(pick[P // 2:P // 2 + 1, :].bitcast(F32), 1.0)
            pool.drain()
            nc.gpsimd.memset(ones[:, :], 1.0).then_inc(consts, 1)

            with pool.Fori(0, CHUNKS) as c:
                pool.wait_ge(pow_wanted, c + 1)
                nc.gpsimd.tensor_tensor(pow_out[:, :, :], pow_in[:, :, :],
                                        neg_half[:, 0:2 * K].rearrange("p (a k) -> p a k", a=2), ALU.pow).then_inc(pow_ready, 1)

            def stage(i, k):
                at = (bass.ds((i * K + k) * P, P) if not isinstance(i, int) else slice((i * K + k) * P, (i * K + k + 1) * P))
                nc.gpsimd.tensor_copy(z_hi_now[:, k, :], z_hi[:, at].bitcast(F32))
                nc.gpsimd.tensor_copy(z_lo_now[:, k, :], z_lo[:, at].bitcast(F32)).then_inc(z_staged, 1)

            def roots(i):
                pool.wait_ge(dist_wanted, i + 1)
                nc.gpsimd.tensor_tensor(dist[:, :, :], dist_in[:, :, :], half[:, :, :], ALU.pow).then_inc(dist_ready, 1)

            def scaled(i, first):
                pool.wait_ge(deg2_wanted, i + 1)
                nc.gpsimd.tensor_tensor(tiles(d2_col, i), sim_deg[:, :], neg_half[:, 0:K], ALU.pow)
                pool.drain()
                if not first:
                    pool.wait_ge(tile_used, i * K)
                    pool.wait_ge(u_stored, i * DMA)
                nc.gpsimd.tensor_tensor(feat_now[:, :, :], tiles(h1, i), over_features(tiles(d2_col, i)),
                                        ALU.mult).then_inc(feat_ready, 1)
                pool.drain()
                pool.dma_start(tiles_of(u_tiles, i), feat_now[:, :, :]).then_inc(u_stored, DMA)
                nc.gpsimd.tensor_copy(tiles(feat_c[0], i), feat_now[:, :, :]).then_inc(feat_c_hi, 1)
                pool.wait_ge(feat_c_hi, i + 1)
                nc.gpsimd.tensor_tensor(tiles(feat_c[1], i), feat_now[:, :, :], tiles(feat_c[0], i).bitcast(F32),
                                        ALU.subtract).then_inc(feat_c_ready, 1)

            def add_b2(i):
                nc.gpsimd.tensor_tensor(tiles(x_sb, i), tiles(x_sb, i), over_tiles(b2_row[:, :]), ALU.add).then_inc(b2_added, 1)

            def step(i, before):
                add_b2(i)
                for k in range(K):
                    pool.wait_ge(pair_ready, (i * K + k + 1) * PAIRS)
                    stage(i + 1, k)
                if before:
                    scaled(i - 1, before == "first")
                roots(i)

            pool.wait_ge(small_in["b2"], DMA)
            pool.wait_ge(z_done, 2)
            for k in range(K):
                stage(0, k)
            pool.wait_ge(z_done, CHUNKS + 1)
            step(0, None)
            step(1, "first")
            with pool.Fori(2, GROUPS - 1) as i:
                step(i, "later")
            add_b2(GROUPS - 1)
            scaled(GROUPS - 2, False)
            roots(GROUPS - 1)
            scaled(GROUPS - 1, False)

            pool.wait_ge(u_stored, GROUPS * DMA)
            def gather(c, slot):
                pool.wait_ge(near_ready, c + 1)
                nc.gpsimd.tensor_copy(idx_now[:, slot, :].rearrange("p (k j) -> p k j", k=K), tiles(near, c)).then_inc(idx_ready, 1)
                wait_apart(pool, idx_ready, c + 1)
                for m in range(K * NEAR):
                    nc.gpsimd.indirect_dma_start(
                        out=gathered[slot][:, m, :], out_offset=None, in_=u_d,
                        in_offset=bass.IndirectOffsetOnAxis(ap=idx_now[:, slot, m:m + 1], axis=0)).then_inc(rows_in[slot][m // NEAR], DMA)

            whole = CHUNKS // ROW_SLOTS
            with pool.Fori(0, whole) as i:
                for slot in range(ROW_SLOTS):
                    gather(i * ROW_SLOTS + slot, slot)
            for c in range(whole * ROW_SLOTS, CHUNKS):
                gather(c, c % ROW_SLOTS)


def kernel(x, adj, L0_gnn_t, L0_gnn_alpha, L0_gnn_W, L0_gnn_b, L1_gnn_W1, L1_gnn_b1, L1_gnn_W2, L1_gnn_b2):
    import numpy as np
    import concourse.bacc as bacc
    from concourse.bass_utils import run_bass_kernel_spmd

    n, h = x.shape
    blocks = np.asarray(adj).T.reshape(n // CHUNK, K, P, n // CHUNK, CHUNK).transpose(3, 0, 2, 1, 4)
    arrays = {
        "x": np.ascontiguousarray(x),
        "at": np.ascontiguousarray(blocks).reshape(n // CHUNK, n // CHUNK, P, K * CHUNK),
        "alpha": np.ascontiguousarray(np.broadcast_to(np.asarray(L0_gnn_alpha).reshape(1, 1), (P, 1))),
        "wt": np.ascontiguousarray(np.asarray(L0_gnn_W).T),
        "b": np.ascontiguousarray(np.broadcast_to(np.asarray(L0_gnn_b), (P, h))),
        "w1": np.ascontiguousarray(L1_gnn_W1),
        "b1": np.ascontiguousarray(np.broadcast_to(np.asarray(L1_gnn_b1), (P, h))),
        "w2": np.ascontiguousarray(L1_gnn_W2),
        "b2": np.ascontiguousarray(np.broadcast_to(np.asarray(L1_gnn_b2), (P, h))),
        "ident": np.eye(P, dtype=np.float32),
    }
    nc = bacc.Bacc("TRN2", target_bir_lowering=False, num_devices=1)
    ins = [nc.dram_tensor(f"in_{k}", a.shape, mybir.dt.from_np(a.dtype), kind="ExternalInput").ap() for k, a in arrays.items()]
    out = nc.dram_tensor("out", (n, h), F32, kind="ExternalOutput").ap()
    scratch = nc.dram_tensor("scaled_features", (n, h), F32, kind="Internal").ap()
    graph_layers(nc, *ins, out, scratch)
    r = run_bass_kernel_spmd(nc, [{f"in_{k}": a for k, a in arrays.items()}], core_ids=[0])
    return r.results[0]["out"]
```
